# Optimizing a Trainium2 kernel written in Bass

```python
import numpy as np
import jax
import jax.numpy as jnp

def _softmax(x, axis=-1):
    return jax.nn.softmax(x, axis=axis)

def _gelu(x):
    return jax.nn.gelu(x, approximate=True)

def _silu(x):
    return jax.nn.silu(x)

def _sigmoid(x):
    return jax.nn.sigmoid(x)

def _layernorm(x, axis=-1, eps=1e-05):
    m = jnp.mean(x, axis=axis, keepdims=True)
    v = jnp.var(x, axis=axis, keepdims=True)
    return (x - m) / jnp.sqrt(v + eps)

def _scatter_add(tgt, idx, src, axis=0):
    return tgt.at[idx].add(src)

def _segment_sum(src, seg, n):
    return jax.ops.segment_sum(src, seg, n)
kernel_name = 'mk_seq_preln_d1_jaxref_r8_545b71'

def setup_inputs(seed: int=0):
    np.random.seed(seed)
    _w = jnp.asarray

    def _L0_attn_setup():
        import jax, jax.numpy as jnp
        import numpy as np
        D_MODEL = 256
        N_HEADS = 16
        HEAD_DIM = D_MODEL // N_HEADS
        SCALE_BASE = 64

        def rotate_half(x):
            x1, x2 = jnp.split(x, 2, axis=-1)
            return jnp.concatenate((-x2, x1), axis=-1)

        def rotary_xpos(seq_len, dim, dtype=jnp.float32):
            inv_freq = 1.0 / 10000.0 ** (jnp.arange(0, dim, 2, dtype=jnp.float32) / dim)
            t = jnp.arange(seq_len, dtype=jnp.float32)
            freqs = jnp.einsum('i,j->ij', t, inv_freq)
            freqs = jnp.concatenate((freqs, freqs), axis=-1)
            scale_base = (jnp.arange(0, dim, 2, dtype=jnp.float32) + 0.4 * dim) / (1.4 * dim)
            power = (t - seq_len // 2) / SCALE_BASE
            scale = scale_base[None, :] ** power[:, None]
            scale = jnp.concatenate((scale, scale), axis=-1)
            return (freqs.astype(dtype), scale.astype(dtype))

        def apply_rotary(t, pos, scale):
            return t * jnp.cos(pos) * scale + rotate_half(t) * jnp.sin(pos) * scale
        key = jax.random.key(seed)
        ks = jax.random.split(key, 5)
        B, S = (2, 256)
        hidden_states = jax.random.normal(ks[0], (B, S, D_MODEL), dtype=jnp.float32)
        w_q = jax.random.normal(ks[1], (N_HEADS * HEAD_DIM, D_MODEL), dtype=jnp.float32) * 0.02
        w_kv = jax.random.normal(ks[2], (2 * HEAD_DIM, D_MODEL), dtype=jnp.float32) * 0.02
        w_proj = jax.random.normal(ks[3], (D_MODEL, N_HEADS * HEAD_DIM), dtype=jnp.float32) * 0.02
        b_proj = jax.random.normal(ks[4], (D_MODEL,), dtype=jnp.float32) * 0.02
        return {'hidden_states': hidden_states, 'w_q': w_q, 'w_kv': w_kv, 'w_proj': w_proj, 'b_proj': b_proj}
    _L0_attn_in = _L0_attn_setup()

    def _L0_ffn_setup():
        import jax, jax.numpy as jnp
        import numpy as np
        NUM_EXPERTS = 64
        HIDDEN = 256
        INTERMEDIATE = 128
        TOP_K = 8
        NORM_TOPK_PROB = False
        key = jax.random.key(seed)
        k1, k2, k3, k4 = jax.random.split(key, 4)
        return {'hidden_states': jax.random.normal(k1, (4, 256, HIDDEN), dtype=jnp.float32), 'router_weight': jax.random.normal(k2, (NUM_EXPERTS, HIDDEN), dtype=jnp.float32) * 0.02, 'gate_up_proj': jax.random.normal(k3, (NUM_EXPERTS, 2 * INTERMEDIATE, HIDDEN), dtype=jnp.float32) * 0.02, 'down_proj': jax.random.normal(k4, (NUM_EXPERTS, HIDDEN, INTERMEDIATE), dtype=jnp.float32) * 0.02}
    _L0_ffn_in = _L0_ffn_setup()
    _d = {'L0_attn_hidden_states': _L0_attn_in['hidden_states'], 'L0_attn_w_q': _L0_attn_in['w_q'], 'L0_attn_w_kv': _L0_attn_in['w_kv'], 'L0_attn_w_proj': _L0_attn_in['w_proj'], 'L0_attn_b_proj': _L0_attn_in['b_proj'], 'L0_ffn_router_weight': _L0_ffn_in['router_weight'], 'L0_ffn_gate_up_proj': _L0_ffn_in['gate_up_proj'], 'L0_ffn_down_proj': _L0_ffn_in['down_proj']}
    _x0 = _d['L0_attn_hidden_states']
    _d['L0_attn_hidden_states'] = jax.random.normal(jax.random.fold_in(jax.random.key(seed), 1), (8, 256, 256), dtype=_x0.dtype)
    del _x0
    return _d

def reference(L0_attn_hidden_states, L0_attn_w_q, L0_attn_w_kv, L0_attn_w_proj, L0_attn_b_proj, L0_ffn_router_weight, L0_ffn_gate_up_proj, L0_ffn_down_proj):

    def _L0_attn_ref(hidden_states, w_q, w_kv, w_proj, b_proj):
        import jax, jax.numpy as jnp
        import numpy as np
        D_MODEL = 256
        N_HEADS = 16
        HEAD_DIM = D_MODEL // N_HEADS
        SCALE_BASE = 64

        def rotate_half(x):
            x1, x2 = jnp.split(x, 2, axis=-1)
            return jnp.concatenate((-x2, x1), axis=-1)

        def rotary_xpos(seq_len, dim, dtype=jnp.float32):
            inv_freq = 1.0 / 10000.0 ** (jnp.arange(0, dim, 2, dtype=jnp.float32) / dim)
            t = jnp.arange(seq_len, dtype=jnp.float32)
            freqs = jnp.einsum('i,j->ij', t, inv_freq)
            freqs = jnp.concatenate((freqs, freqs), axis=-1)
            scale_base = (jnp.arange(0, dim, 2, dtype=jnp.float32) + 0.4 * dim) / (1.4 * dim)
            power = (t - seq_len // 2) / SCALE_BASE
            scale = scale_base[None, :] ** power[:, None]
            scale = jnp.concatenate((scale, scale), axis=-1)
            return (freqs.astype(dtype), scale.astype(dtype))

        def apply_rotary(t, pos, scale):
            return t * jnp.cos(pos) * scale + rotate_half(t) * jnp.sin(pos) * scale
        B, S, _ = hidden_states.shape
        q = hidden_states @ w_q.T
        kv = hidden_states @ w_kv.T
        k, v = jnp.split(kv, 2, axis=-1)
        q = q.reshape(B, S, N_HEADS, HEAD_DIM).transpose(0, 2, 1, 3)
        scale_w = HEAD_DIM ** (-0.5)
        q = q * scale_w
        k = k * scale_w
        pos, xscale = rotary_xpos(S, HEAD_DIM, q.dtype)
        q = apply_rotary(q, pos, xscale)
        k = apply_rotary(k, pos, 1.0 / xscale)
        attn = jnp.einsum('bnih,bjh->bnij', q, k)
        causal = jnp.triu(jnp.ones((S, S), dtype=bool), 1)
        attn = jnp.where(causal, -jnp.finfo(attn.dtype).max, attn)
        attn = jax.nn.softmax(attn, axis=-1)
        out = jnp.einsum('bnij,bjd->bind', attn, v)
        out = out.reshape(B, S, N_HEADS * HEAD_DIM)
        out = out @ w_proj.T + b_proj
        return out

    def _L0_ffn_ref(hidden_states, router_weight, gate_up_proj, down_proj):
        import jax, jax.numpy as jnp
        import numpy as np
        NUM_EXPERTS = 64
        HIDDEN = 256
        INTERMEDIATE = 128
        TOP_K = 8
        NORM_TOPK_PROB = False
        B, L, H = hidden_states.shape
        x = hidden_states.reshape(-1, H)
        T = x.shape[0]
        logits = x @ router_weight.T
        probs = jax.nn.softmax(logits.astype(jnp.float32), axis=-1)
        top_v, top_i = jax.lax.top_k(probs, TOP_K)
        if NORM_TOPK_PROB:
            top_v = top_v / jnp.sum(top_v, axis=-1, keepdims=True)
        comb = jnp.zeros((T, NUM_EXPERTS), dtype=probs.dtype)
        comb = comb.at[jnp.arange(T)[:, None], top_i].add(top_v)

        def body(acc, inputs):
            w_gu, w_d, c = inputs
            gate, up = jnp.split(x @ w_gu.T, 2, axis=-1)
            y = jax.nn.silu(gate) * up @ w_d.T
            return (acc + c[:, None] * y, None)
        out, _ = jax.lax.scan(body, jnp.zeros_like(x), (gate_up_proj, down_proj, comb.T))
        return out.reshape(B, L, H)
    x = L0_attn_hidden_states
    x = x + _L0_attn_ref(_layernorm(x, axis=-1), L0_attn_w_q, L0_attn_w_kv, L0_attn_w_proj, L0_attn_b_proj)
    x = x + _L0_ffn_ref(_layernorm(x, axis=-1), L0_ffn_router_weight, L0_ffn_gate_up_proj, L0_ffn_down_proj)
    return x

_drawn_inputs = setup_inputs


def setup_inputs(seed=0):
    import zlib

    import numpy as np

    out = dict(_drawn_inputs(seed))
    spreads = {}
    factors = {'L0_attn_w_q': 8.0,
     'L0_attn_w_kv': 3.693,
     'L0_attn_w_proj': 3.685,
     'L0_attn_b_proj': 2.909,
     'L0_ffn_router_weight': 8.0,
     'L0_ffn_gate_up_proj': 8.0,
     'L0_ffn_down_proj': 8.0}
    for name, (base, spread) in spreads.items():
        noise = np.random.default_rng([zlib.crc32(name.encode()), seed]).standard_normal(out[name].shape)
        drawn = base * np.exp(spread * noise) if base else spread * noise
        out[name] = jnp.asarray(drawn.astype(out[name].dtype))
    for name, factor in factors.items():
        out[name] = (out[name] * factor).astype(out[name].dtype)
    return out
```

```python
from contextlib import ExitStack

import concourse.bass as bass
from concourse import mybir
from concourse.alu_op_type import AluOpType as ALU

ACT = mybir.ActivationFunctionType
AX = mybir.AxisListType
F32 = mybir.dt.float32
BF16 = mybir.dt.bfloat16
I32 = mybir.dt.int32
U32 = mybir.dt.uint32

P = 128
B, S, D = 8, 256, 256
T = B * S
TT = T // P
NT = S // P
H, HD = 16, 16
G = P // HD
QK = H * HD + HD
QKV = QK + HD
E, TOPK, F = 64, 8, 128
EPS = 1e-5
MASKED = -3.0e38
RSQRT_SEED = float(0x5F3759DF)

U = 12
VW = HD + 1

SLOTS = NT * P
PAD = SLOTS
REGION = PAD + T
ID, PR = D, D + 1
ROW = D + 1 + E
WCOLS = 2 * 2 * F + D
OVER = max(min(k * ((T - SLOTS) // P), (T * TOPK - k * SLOTS + k * (P - 1)) // P) for k in range(1, E + 1))
NB = 8
OVW = -(-(OVER + 2) // NB) * NB


def unit_shape(u):
    return (0, 4 * u, 4, P) if u < 4 else (1, 2 * (u - 4), 2, S)


def wait(eng, sem, value):
    if isinstance(value, int) and value <= 0:
        return
    eng.wait_ge(sem, value)


def moe_block(nc, x, wqkv, wproj, bproj, wrouter, wexpert, cos_t, sin_t, consts, out, rows, acc0, acc1):
    acc = (acc0, acc1)
    with ExitStack() as ctx:
        def sb(name, shape, dt=F32):
            return ctx.enter_context(nc.sbuf_tensor(name, shape, dt))

        def sem(name):
            return ctx.enter_context(nc.semaphore(name))

        tri = sb("tri", [P, P], BF16)
        ident_bf = sb("ident_bf", [P, P], BF16)
        mask_bf = sb("mask_bf", [P, 4, P], BF16)
        ones_bf = sb("ones_bf", [P, P], BF16)
        ones = sb("ones", [P, 1])
        consts_sb = sb("consts_sb", [P, 3 * P + G + E + 1 + NT])
        ident, tri_f, mask_f = (consts_sb[:, k * P:(k + 1) * P] for k in range(3))
        head_mask = consts_sb[:, 3 * P:3 * P + G]
        region_row = consts_sb[:, 3 * P + G:3 * P + G + E]
        region_col = consts_sb[:, 3 * P + G + E:3 * P + G + E + 1]
        token0 = consts_sb[:, 3 * P + G + E + 1:3 * P + G + E + 1 + NT]
        wqkv_sb = sb("wqkv_sb", [P, 2, QKV])
        wproj_sb = sb("wproj_sb", [P, 2, D])
        wrouter_sb = sb("wrouter_sb", [P, 2, E])
        bias_sb = sb("bias_sb", [P, D])
        cos_sb = sb("cos_sb", [P, NT, QK])
        sin_sb = sb("sin_sb", [P, NT, QK])
        x_sb = sb("x_sb", [P, 2, NT, D])
        stats = sb("stats", [P, NT, 6])
        mv = sb("mv", [P, NT, 2])
        var = sb("var", [P, NT])
        rstd = sb("rstd", [P, NT])
        guess = sb("guess", [P, NT])
        xn = sb("xn", [P, NT, D])
        xnT = sb("xnT", [P, 2, S])
        rot_a = sb("rot_a", [P, NT, QK])
        rot_b = sb("rot_b", [P, NT, QK])
        qk = sb("qk", [P, NT, QK])
        krep = sb("krep", [P, NT, G, HD])
        qT = sb("qT", [P, 2, 2, S])
        kbd = sb("kbd", [P, 2, G, S])
        v1 = sb("v1", [P, 2, NT, VW])
        neg_max = sb("neg_max", [P, 2, 4])
        probs = sb("probs", [P, 2, 512])
        pT = sb("pT", [P, 2, 512])
        rden = sb("rden", [P, H])
        attn = sb("attn", [P, NT, D])
        attnT = sb("attnT", [P, 2, S])
        xb = sb("xb", [P, 2, NT, D])
        x2 = sb("x2", [P, 2, NT, D])
        token = sb("token", [P, NT])
        row_sb = sb("row_sb", [P, 2, NT, ROW])
        xn2T = sb("xn2T", [P, 2, S])
        neg_top = sb("neg_top", [P, NT])
        esum = sb("esum", [P, NT])
        eprob = sb("eprob", [P, NT, E])
        top8 = sb("top8", [P, NT, TOPK])
        marked = sb("marked", [P, NT, E])
        chosen = sb("chosen", [P, NT, E], BF16)
        next_row = sb("next_row", [P, E])
        slot = sb("slot", [P, NT, E])
        slot8 = sb("slot8", [P, NT, TOPK])
        slot_ix = sb("slot_ix", [P, 2, NT, TOPK], U32)
        zeros = sb("zeros", [P, 2, ROW])
        n_row = sb("n_row", [1, E])
        over_i = sb("over_i", [E, 1], I32)
        over = sb("over", [E, 1])
        over_end = sb("over_end", [E, 1])
        over_start = sb("over_start", [E, 1])
        over_base = sb("over_base", [E, 1])
        tile_no = sb("tile_no", [E, OVW])
        ended = sb("ended", [E, OVW])
        begun = sb("begun", [E, OVW])
        table = sb("table", [1, 1 + E + 2 * OVW], I32)
        row_tmp = sb("row_tmp", [1, OVW])
        N_OVER, MAIN, OV_E, OV_ROW = 0, 1, 1 + E, 1 + E + OVW
        w_sb = sb("w_sb", [P, NB, WCOLS])
        xt = sb("xt", [P, NB, NT, ROW])
        xtT = sb("xtT", [P, 2, 2, SLOTS])
        pcol = sb("pcol", [P, NB, NT])
        gate = sb("gate", [P, 2, SLOTS])
        hid = sb("hid", [P, 2, SLOTS])
        y = sb("y", [P, NB, NT, D])
        fin_a = sb("fin_a", [P, 2, 4, D])
        fin_b = sb("fin_b", [P, 2, 4, D])
        fin_sum = sb("fin_sum", [P, 2, 4, D])

        psA = ctx.enter_context(nc.psum_tensor("psA", [P, 512], F32))
        psB = ctx.enter_context(nc.psum_tensor("psB", [P, 512], F32))
        psC = ctx.enter_context(nc.psum_tensor("psC", [P, 512], F32))
        psO = ctx.enter_context(nc.psum_tensor("psO", [P, 512], F32))
        psS = [ctx.enter_context(nc.psum_tensor(f"psS{i}", [P, 512], F32)) for i in range(2)]
        psT = [ctx.enter_context(nc.psum_tensor(f"psT{i}", [P, 512], F32)) for i in range(2)]
        psX, psG, psY = [psA, psB], psS, [psT, [psC, psO]]

        ld_const = sem("ld_const")
        ld_x = [sem(f"ld_x{i}") for i in range(2)]
        made_ones = sem("made_ones")
        made_consts = sem("made_consts")
        made_zero = sem("made_zero")
        zero_stored = sem("zero_stored")
        xn_ready, xnT_in, xnT_ready, qkv_ready = (sem(n) for n in ("xn_ready", "xnT_in", "xnT_ready", "qkv_ready"))
        v_ready, rot_ready, qk_ready = (sem(n) for n in ("v_ready", "rot_ready", "qk_ready"))
        qkT_in, qT_ready, kbd_ready, xb_ready = (sem(n) for n in ("qkT_in", "qT_ready", "kbd_ready", "xb_ready"))
        scores_ready, max_ready, probs_ready = (sem(n) for n in ("scores_ready", "max_ready", "probs_ready"))
        pT_in, pT_act, pT_dve, pv_done = (sem(n) for n in ("pT_in", "pT_act", "pT_dve", "pv_done"))
        attn_ready = sem("attn_ready")
        attnT_in, attnT_ready, proj_ready, x2_ready = (sem(n) for n in ("attnT_in", "attnT_ready", "proj_ready", "x2_ready"))
        x2_stored = [sem(f"x2_stored{i}") for i in range(2)]
        xn2_ready, xn2T_in, xn2T_ready, logits_ready = (sem(n) for n in ("xn2_ready", "xn2T_in", "xn2T_ready", "logits_ready"))
        top_ready, exp_ready, chosen_ready = (sem(n) for n in ("top_ready", "exp_ready", "chosen_ready"))
        rank_ready, slots_ready = sem("rank_ready"), sem("slots_ready")
        sent = [[sem(f"sent{p}{t}") for t in range(NT)] for p in range(2)]
        pool_go = sem("pool_go")
        tb_dve, tb_pe, table_ready = sem("tb_dve"), sem("tb_pe"), sem("table_ready")
        w_loaded = [sem(f"w_loaded{j}") for j in range(NB)]
        x_loaded = [sem(f"x_loaded{j}") for j in range(NB)]
        xtT_in, xtT_ready, pcol_ready = sem("xtT_in"), sem("xtT_ready"), sem("pcol_ready")
        gu_ready, gate_ready, hid_ready, down_ready = (sem(n) for n in ("gu_ready", "gate_ready", "hid_ready", "down_ready"))
        y_dve, y_act = sem("y_dve"), sem("y_act")
        added = [sem(f"added{j}") for j in range(NB)]
        all_added = sem("all_added")
        fin_loaded = [sem(f"fin_loaded{j}") for j in range(2)]
        fin_ready = sem("fin_ready")
        fin_stored = [sem(f"fin_stored{j}") for j in range(2)]

        block = ctx.enter_context(nc.Block())

        N_LD_CONST = 7


        def after(i, h, par):
            return (i + 1, h + 1, 0) if par else (i + 1, h, 1)

        def before(i, h, par):
            return (i - 1, h, 0) if par else (i - 1, h - 1, 1)

        def nothing(*_):
            pass

        def run_phase1(eng, step=nothing, stage1=nothing, stage3=nothing):
            def batch(b, first=False, last=False):
                for s in range(U + 2):
                    step(*b, s)
                    if s % 2 == 0 and s // 2 < 5 and not first:
                        stage3(*before(*b), s // 2)
                    if s % 2 == 1 and s // 2 < 4 and not last:
                        stage1(*after(*b), s // 2)

            for piece in range(4):
                stage1(0, 0, 0, piece)
            batch((0, 0, 0), first=True)
            with eng.Fori(0, (B - 2) // 2) as it:
                batch((it * 2 + 1, it, 1))
                batch((it * 2 + 2, it + 1, 0))
            batch((B - 1, (B - 1) // 2, 1), last=True)
            for piece in range(5):
                stage3(B - 1, (B - 1) // 2, 1, piece)

        def run_phase2(eng, load=nothing, up=nothing, down=nothing):
            def main(m, q, j):
                if not isinstance(m, int) or m < E:
                    load(m, q, j, NT, m, None)
                if not isinstance(m, int) or 1 <= m <= E:
                    up(m - 1, q if j >= 1 else q - 1, (j - 1) % NB, NT)
                if not isinstance(m, int) or 2 <= m:
                    down(m - 2, q if j >= 2 else q - 1, (j - 2) % NB, NT)

            for m in range(NB):
                main(m, 0, m)
            with eng.Fori(1, E // NB) as q:
                for j in range(NB):
                    main(q * NB + j, q, j)
            for m in range(E, E + 2):
                main(m, m // NB, m % NB)
            if load is nothing and up is nothing and down is nothing:
                return
            n_over = eng.value_load(table[0:1, N_OVER:N_OVER + 1], min_val=0, max_val=OVER)

            def extra(m, q, j):
                if load is not nothing and (not isinstance(m, int) or m < OVER):
                    with eng.If(n_over > m):
                        load(m + E, q + E // NB, j, 1, None, m)
                if up is not nothing and (not isinstance(m, int) or m >= 1):
                    with eng.If(n_over > m - 1):
                        up(m + (E - 1), (q if j >= 1 else q - 1) + E // NB, (j - 1) % NB, 1)
                if down is not nothing and (not isinstance(m, int) or m >= 2):
                    with eng.If(n_over > m - 2):
                        down(m + (E - 2), (q if j >= 2 else q - 1) + E // NB, (j - 2) % NB, 1)

            for m in range(NB):
                extra(m, 0, m)
            with eng.Fori(1, OVW // NB) as q:
                with eng.If(n_over > q * NB - 2):
                    for j in range(NB):
                        extra(q * NB + j, q, j)

        def adds_before(q, j, nsub):
            return q * (16 * NT) if nsub == NT else (q - E // NB) * 16 + E // NB * 16 * NT

        def rows_of(dram, r0, n):
            return dram[bass.ds(r0, n * P), :].rearrange("(a p) n -> p a n", p=P)

        @block.sync
        def _(sp):
            sp.dma_start(consts_sb[:], consts[:, :]).then_inc(ld_const, 16)
            sp.dma_start(wqkv_sb[:], wqkv.rearrange("(c p) n -> p c n", p=P)).then_inc(ld_const, 16)

            def load_x(i, h, par):
                wait(sp, xn_ready, i - 1)
                wait(sp, xb_ready, i - 1)
                sp.dma_start(x_sb[:, par, :, :], rows_of(x, i * S, NT)).then_inc(ld_x[par], 16)

            load_x(0, 0, 0)
            sp.dma_start(cos_sb[:], cos_t.rearrange("(a p) n -> p a n", p=P)).then_inc(ld_const, 16)
            sp.dma_start(sin_sb[:], sin_t.rearrange("(a p) n -> p a n", p=P)).then_inc(ld_const, 16)
            sp.dma_start(bias_sb[:], bproj.partition_broadcast(P)).then_inc(ld_const, 16)
            sp.dma_start(wproj_sb[:], wproj.rearrange("(c p) n -> p c n", p=P)).then_inc(ld_const, 16)
            sp.dma_start(wrouter_sb[:], wrouter.rearrange("(c p) n -> p c n", p=P)).then_inc(ld_const, 16)
            load_x(1, 0, 1)

            sp.wait_ge(made_zero, 1 + NT)
            for a in range((T + PAD) // PAD):
                sp.dma_start(rows_of(acc[1], a * PAD, NT), zeros[:, :, 0:D]).then_inc(zero_stored, 16)
            sp.dma_start(rows_of(acc[0], T, NT), zeros[:, :, 0:D]).then_inc(zero_stored, 16)
            with sp.Fori(0, E) as e:
                sp.dma_start(rows_of(rows, e * REGION, NT), zeros[:]).then_inc(zero_stored, 16)

            def stage1(i, h, par, piece):
                if piece == 0 and not (isinstance(i, int) and i <= 1):
                    load_x(i, h, par)

            def stage3(i, h, par, piece):
                if piece == 1:
                    sp.wait_ge(x2_ready, i + 1)
                    sp.dma_start(rows_of(acc[0], i * S, NT), x2[:, par, :, :]).then_inc(x2_stored[par], 16)

            run_phase1(sp, stage1=stage1, stage3=stage3)

            for p in range(2):
                for t in range(NT):
                    sp.wait_ge(sent[p][t], B // 2 * TOPK * 16)
            sp.wait_ge(zero_stored, ((T + PAD) // PAD + 1 + E) * 16)
            sp.wait_ge(table_ready, 1)

            def load(n, q, j, nsub, e, extra_no):
                if e is None:
                    e = sp.value_load(table[0:1, bass.ds(extra_no + OV_E, 1)], min_val=0, max_val=E - 1)
                    r0 = sp.value_load(table[0:1, bass.ds(extra_no + OV_ROW, 1)], min_val=0,
                                       max_val=E * REGION - P)
                else:
                    r0 = sp.value_load(table[0:1, bass.ds(e + MAIN, 1)], min_val=0,
                                       max_val=E * REGION - SLOTS)
                wait(sp, added[j], adds_before(q, j, nsub))
                sp.dma_start(xt[:, j, 0:nsub, :], rows_of(rows, r0, nsub)).then_inc(x_loaded[j], 16)
                wait(sp, down_ready, n - (NB - 1))
                sp.dma_start(w_sb[:, j, :], wexpert[bass.ds(e * P, P), :]).then_inc(w_loaded[j], 16)

            run_phase2(sp, load=load)

            sp.wait_ge(all_added, 1)
            for i in range(TT // 4):
                wait(sp, fin_ready, i - 1)
                for a, buf in ((0, fin_a), (1, fin_b)):
                    sp.dma_start(buf[:, i % 2, :, :], rows_of(acc[a], i * 4 * P, 4)).then_inc(fin_loaded[i % 2], 16)

        @block.gpsimd
        def _(pool):
            nc.gpsimd.memset(zeros[:], 0.0).then_inc(made_zero, 1)
            nc.gpsimd.memset(v1[:], 1.0).then_inc(made_ones, 1)
            nc.gpsimd.memset(ones[:], 1.0).then_inc(made_ones, 1)
            nc.gpsimd.memset(ones_bf[:], 1.0).then_inc(made_ones, 1)
            nc.gpsimd.iota(tile_no[:], [[1, OVW]], base=0, channel_multiplier=0,
                           allow_small_or_imprecise_dtypes=True).then_inc(made_ones, 1)
            pool.wait_ge(made_zero, 1)
            for a in range(NT):
                nc.gpsimd.iota(zeros[:, a, ID:ID + 1].bitcast(I32), [[0, 1]], base=T + a * P,
                               channel_multiplier=1).then_inc(made_zero, 1)
            pool.wait_ge(ld_const, N_LD_CONST * 16)

            def stage1(i, h, par, piece):
                if piece == 0:
                    pool.wait_ge(ld_x[par], h * 16 + 16)
                    wait(pool, x2_ready, i - 1)
                    nc.gpsimd.tensor_tensor(xb[:, par, :, :], x_sb[:, par, :, :],
                                            bias_sb[:].unsqueeze(1).to_broadcast([P, NT, D]),
                                            ALU.add).then_inc(xb_ready, 1)
                if piece == 2:
                    wait(pool, qkT_in, i)
                    for t in range(NT):
                        pool.wait_ge(rot_ready, i * NT + (t + 1))
                        nc.gpsimd.tensor_tensor(qk[:, t, :], rot_a[:, t, :], rot_b[:, t, :], ALU.add)
                        key_a, key_b = (r[:, t, H * HD:QK].unsqueeze(1).to_broadcast([P, G, HD])
                                        for r in (rot_a, rot_b))
                        nc.gpsimd.tensor_tensor(krep[:, t, :, :], key_a, key_b, ALU.add).then_inc(qk_ready, 1)

            def stage3(i, h, par, piece):
                if piece == 4:
                    pool.wait_ge(slots_ready, i + 1)
                    pool.sem_inc(pool_go, 1)
                    for t in range(NT):
                        for k in range(TOPK):
                            nc.gpsimd.indirect_dma_start(
                                rows, bass.IndirectOffsetOnAxis(ap=slot_ix[:, par, t, k:k + 1], axis=0),
                                row_sb[:, par, t, :], None).then_inc(sent[par][t], 16)

            run_phase1(pool, stage1=stage1, stage3=stage3)
            pool.wait_ge(table_ready, 1)
            for par in range(2):
                pool.wait_ge(x2_stored[par], B // 2 * 16)
            pool.wait_ge(zero_stored, ((T + PAD) // PAD + 1 + E) * 16)

            def down(n, q, j, nsub):
                pool.wait_ge(y_dve, n + 1)
                if nsub == NT:
                    pool.wait_ge(y_act, n + 1)
                wait(pool, added[(j - 2) % NB], adds_before(q + 1 if j >= 2 else q, j, nsub))
                pool.sem_inc(pool_go, 1)
                for a in range(nsub):
                    nc.gpsimd.indirect_dma_start(
                        acc[j % 2], bass.IndirectOffsetOnAxis(ap=xt[:, j, a, ID:ID + 1].bitcast(U32), axis=0),
                        y[:, j, a, :], None, compute_op=ALU.add).then_inc(added[j], 16)

            run_phase2(pool, down=down)
            n_over = pool.value_load(table[0:1, N_OVER:N_OVER + 1], min_val=0, max_val=OVER)
            for j in range(NB):
                pool.wait_ge(added[j], (n_over + (NB - 1 - j)) // NB * 16 + E // NB * 16 * NT)
            pool.sem_inc(all_added, 1)

        @block.scalar
        def _(act):
            act.wait_ge(made_ones, 4)

            def step(i, h, par, s):
                if s < U:
                    n, (t, h0, nh, nk) = i * U + s, unit_shape(s)
                    act.wait_ge(max_ready, n + 1)
                    wait(act, pT_in, n - 1)
                    for k in range(nh):
                        last = nc.scalar.activation(probs[:, s % 2, k * nk:(k + 1) * nk],
                                                    psS[s % 2][:, k * nk:(k + 1) * nk], ACT.Exp,
                                                    bias=neg_max[:, s % 2, k:k + 1])
                    last.then_inc(probs_ready, 1)
                if 1 <= s <= U and (s - 1) % 2 == 1:
                    n = i * U + (s - 1)
                    act.wait_ge(pT_in, n + 1)
                    wait(act, pv_done, n - 1)
                    nc.scalar.copy(pT[:, 1, :], psT[1][:]).then_inc(pT_act, 1)

            def stage1(i, h, par, piece):
                if piece == 1:
                    act.wait_ge(xnT_in, i + 1)
                    wait(act, qkv_ready, i * NT)
                    nc.scalar.copy(xnT[:].rearrange("p c n -> p (c n)"), psA[:]).then_inc(xnT_ready, 1)
                if piece == 3:
                    act.wait_ge(qkT_in, i + 1)
                    wait(act, scores_ready, (i - 1) * U)
                    nc.scalar.copy(qT[:, par, :, :].rearrange("p c n -> p (c n)"), psA[:]).then_inc(qT_ready, 1)

            def stage3(i, h, par, piece):
                if piece == 0:
                    act.wait_ge(attnT_in, i + 1)
                    wait(act, proj_ready, i)
                    nc.scalar.copy(attnT[:].rearrange("p c n -> p (c n)"), psC[:]).then_inc(attnT_ready, 1)
                if piece == 2:
                    act.wait_ge(xn2T_in, i + 1)
                    wait(act, logits_ready, i)
                    nc.scalar.copy(xn2T[:].rearrange("p c n -> p (c n)"), psC[:]).then_inc(xn2T_ready, 1)
                if piece == 3:
                    act.wait_ge(top_ready, i + 1)
                    for t in range(NT):
                        last = nc.scalar.activation(eprob[:, t, :], psC[:, t * E:(t + 1) * E], ACT.Exp,
                                                    bias=neg_top[:, t:t + 1], accum_out=esum[:, t:t + 1])
                    last.then_inc(exp_ready, 1)

            run_phase1(act, step, stage1, stage3)
            act.wait_ge(table_ready, 1)

            def load(n, q, j, nsub, e, extra_no):
                act.wait_ge(xtT_in, n + 1)
                wait(act, gu_ready, n - 1)
                nc.scalar.copy(xtT[:, j % 2, :, 0:nsub * P],
                               psX[j % 2][:].rearrange("p (c n) -> p c n", c=2)[:, :, 0:nsub * P]
                               ).then_inc(xtT_ready, 1)

            def up(n, q, j, nsub):
                act.wait_ge(gu_ready, n + 1)
                wait(act, hid_ready, n - 1)
                nc.scalar.activation(gate[:, j % 2, 0:nsub * P], psG[j % 2][:, 0:nsub * P],
                                     ACT.Silu).then_inc(gate_ready, 1)

            def down(n, q, j, nsub):
                if nsub == NT:
                    act.wait_ge(down_ready, n + 1)
                    act.wait_ge(pcol_ready, n + 1)
                    nc.scalar.mul(y[:, j, 1, :], psY[1][j % 2][:, 0:D], pcol[:, j, 1:2]).then_inc(y_act, 1)

            run_phase2(act, load, up, down)

            for i in range(TT // 4):
                act.wait_ge(fin_ready, i + 1)
                act.dma_start(rows_of(out, i * 4 * P, 4), fin_sum[:, i % 2, :, :]).then_inc(fin_stored[i % 2], 16)
            for j in range(2):
                act.wait_ge(fin_stored[j], TT // 8 * 16)

        @block.vector
        def _(dve):
            v = nc.vector

            def layernorm(source, result, signal):
                for t in range(NT):
                    v.bn_stats(stats[:, t, :], source[:, t, :])
                dve.drain()
                for t in range(NT):
                    v.bn_aggr(mv[:, t, :], stats[:, t, :])
                dve.drain()
                v.tensor_scalar(var[:], mv[:, :, 1], EPS, None, ALU.add)
                dve.drain()
                v.tensor_scalar(guess[:].bitcast(I32), var[:].bitcast(I32), 1, None, ALU.logical_shift_right)
                dve.drain()
                v.tensor_scalar(rstd[:].bitcast(I32), guess[:].bitcast(I32), -1.0, RSQRT_SEED, ALU.mult, ALU.add)
                for _ in range(4):
                    dve.drain()
                    v.tensor_tensor(guess[:], rstd[:], rstd[:], ALU.mult)
                    dve.drain()
                    v.scalar_tensor_tensor(guess[:], guess[:], -0.5, var[:], ALU.mult, ALU.mult)
                    dve.drain()
                    v.scalar_tensor_tensor(rstd[:], guess[:], 1.5, rstd[:], ALU.add, ALU.mult)
                dve.drain()
                for t in range(NT):
                    last = v.tensor_scalar(result[:, t, 0:D], source[:, t, :], mv[:, t, 0:1], rstd[:, t:t + 1],
                                           ALU.subtract, ALU.mult)
                last.then_inc(signal, 1)

            dve.wait_ge(ld_const, N_LD_CONST * 16)
            dve.wait_ge(made_ones, 4)
            v.tensor_copy(tri[:], tri_f)
            v.tensor_copy(ident_bf[:], ident)
            v.tensor_copy(mask_bf[:], mask_f.unsqueeze(1).to_broadcast([P, 4, P]))
            v.tensor_copy(token[:], token0)
            v.tensor_copy(next_row[:], region_row).then_inc(made_consts, 1)

            def step(i, h, par, s):
                if s < U:
                    n, (t, h0, nh, nk) = i * U + s, unit_shape(s)
                    dve.wait_ge(scores_ready, n + 1)
                    wait(dve, probs_ready, n - 1)
                    v.reduce_max(neg_max[:, s % 2, 0:nh], psS[s % 2][:].rearrange("p (h k) -> p h k", h=nh),
                                 AX.X, negate=True).then_inc(max_ready, 1)
                if 1 <= s <= U and (s - 1) % 2 == 0:
                    n = i * U + (s - 1)
                    dve.wait_ge(pT_in, n + 1)
                    wait(dve, pv_done, n - 1)
                    v.tensor_copy(pT[:, 0, :], psT[0][:]).then_inc(pT_dve, 1)
                if s in (6, U + 1):
                    t = 0 if s == 6 else 1
                    dve.wait_ge(pv_done, i * U + (4 if t == 0 else U))
                    wait(dve, attnT_in, i)
                    heads = psO[:, 0:H * VW].rearrange("p (h w) -> p h w", w=VW)
                    v.reciprocal(rden[:].unsqueeze(2), heads[:, :, HD:VW])
                    dve.drain()
                    v.tensor_tensor(attn[:, t, :].rearrange("p (h w) -> p h w", w=HD), heads[:, :, 0:HD],
                                    rden[:].unsqueeze(2).to_broadcast([P, H, HD]), ALU.mult).then_inc(attn_ready, 1)

            def stage1(i, h, par, piece):
                if piece == 0:
                    dve.wait_ge(ld_x[par], h * 16 + 16)
                    wait(dve, xnT_in, i)
                    layernorm(x_sb[:, par, :, :], xn, xn_ready)
                if piece == 2:
                    wait(dve, qk_ready, i * NT)
                    wait(dve, pv_done, (i - 1) * U)
                    for t in range(NT):
                        dve.wait_ge(qkv_ready, i * NT + (t + 1))
                        ps = (psB, psA)[t][:, 0:QK]
                        v.tensor_tensor(rot_a[:, t, :], ps, cos_sb[:, t, :], ALU.mult)
                        halves = ps.rearrange("p (h two e) -> p h two e", two=2, e=HD // 2)
                        turned = rot_b[:, t, :].rearrange("p (h two e) -> p h two e", two=2, e=HD // 2)
                        sines = sin_sb[:, t, :].rearrange("p (h two e) -> p h two e", two=2, e=HD // 2)
                        for w in range(2):
                            last = v.tensor_tensor(turned[:, :, w, :], halves[:, :, 1 - w, :],
                                                   sines[:, :, w, :], ALU.mult)
                        last.then_inc(rot_ready, 1)
                        v.tensor_copy(v1[:, par, t, 0:HD], (psB, psA)[t][:, QK:QKV]).then_inc(v_ready, 1)
                if piece == 3:
                    dve.wait_ge(qkT_in, i + 1)
                    wait(dve, scores_ready, (i - 1) * U)
                    v.tensor_tensor(kbd[:, par, :, :], psB[:, 0:S].unsqueeze(1).to_broadcast([P, G, S]),
                                    head_mask.unsqueeze(2).to_broadcast([P, G, S]), ALU.mult).then_inc(kbd_ready, 1)

            def stage3(i, h, par, piece):
                if piece == 1:
                    dve.wait_ge(proj_ready, i + 1)
                    dve.wait_ge(xb_ready, i + 1)
                    wait(dve, x2_stored[par], h * 16)
                    v.tensor_tensor(x2[:, par, :, :], psC[:].rearrange("p (t n) -> p t n", t=NT),
                                    xb[:, par, :, :], ALU.add).then_inc(x2_ready, 1)
                    for t in range(NT):
                        wait(dve, sent[par][t], h * (TOPK * 16))
                    v.tensor_copy(row_sb[:, par, :, ID].bitcast(I32), token[:])
                    dve.drain()
                    v.tensor_scalar(token[:], token[:], float(S), None, ALU.add)
                    layernorm(x2[:, par, :, :], row_sb[:, par, :, :], xn2_ready)
                if piece == 3:
                    dve.wait_ge(logits_ready, i + 1)
                    v.reduce_max(neg_top[:], psC[:, 0:NT * E].rearrange("p (t e) -> p t e", t=NT), AX.X,
                                 negate=True).then_inc(top_ready, 1)
                    dve.wait_ge(exp_ready, i + 1)
                    v.reciprocal(esum[:], esum[:])
                    dve.drain()
                    pr = row_sb[:, par, :, PR:PR + E]
                    v.tensor_tensor(pr, eprob[:], esum[:].unsqueeze(2).to_broadcast([P, NT, E]), ALU.mult)
                    dve.drain()
                    for t in range(NT):
                        v.max(top8[:, t, :], pr[:, t, :])
                    dve.drain()
                    for t in range(NT):
                        v.match_replace(marked[:, t, :], top8[:, t, :], pr[:, t, :], -1.0)
                    dve.drain()
                    v.tensor_scalar(chosen[:], marked[:], 0.0, None, ALU.is_lt).then_inc(chosen_ready, 1)
                if piece == 4:
                    dve.wait_ge(rank_ready, i + 1)
                    for t in range(NT):
                        ranks = psC[:, (1 + t) * 2 * E:(2 + t) * 2 * E]
                        v.tensor_tensor(slot[:, t, :], ranks[:, 0:E], next_row[:], ALU.add)
                        dve.drain()
                        v.tensor_tensor(next_row[:], next_row[:], ranks[:, E:2 * E], ALU.add)
                        v.tensor_tensor(slot[:, t, :], slot[:, t, :], chosen[:, t, :], ALU.mult)
                        dve.drain()
                        v.max(slot8[:, t, :], slot[:, t, :])
                    dve.drain()
                    v.tensor_copy(slot_ix[:, par, :, :], slot8[:]).then_inc(slots_ready, 1)

            run_phase1(dve, step, stage1, stage3)

            v.tensor_tensor(n_row[:], next_row[0:1, :], region_row[0:1, :], ALU.subtract).then_inc(tb_dve, 1)
            dve.wait_ge(tb_pe, 1)
            v.tensor_scalar(over[:], psA[0:E, 0:1], -float(SLOTS), 0.0, ALU.add, ALU.max)
            dve.drain()
            v.tensor_scalar(over_i[:], over[:], float(P - 1), None, ALU.add)
            dve.drain()
            v.tensor_scalar(over_i[:], over_i[:], P.bit_length() - 1, None, ALU.logical_shift_right)
            dve.drain()
            v.tensor_scalar(over_base[:], psA[0:E, 0:1], region_col[0:E, :], -float(SLOTS + P), ALU.add, ALU.add)
            v.tensor_copy(over[:], over_i[:]).then_inc(tb_dve, 1)
            dve.wait_ge(tb_pe, 2)
            v.tensor_copy(over_start[:], psA[0:E, 2:3])
            dve.drain()
            v.tensor_tensor(over_end[:], over_start[:], over[:], ALU.add)
            v.scalar_tensor_tensor(over_base[:], over_start[:], float(P), over_base[:], ALU.mult, ALU.add)
            dve.drain()
            v.tensor_scalar(ended[:], tile_no[:], over_end[:, 0:1], None, ALU.is_ge)
            v.tensor_scalar(begun[:], tile_no[:], over_start[:, 0:1], None, ALU.is_ge)
            dve.drain()
            v.tensor_tensor(begun[:], begun[:], ended[:], ALU.subtract).then_inc(tb_dve, 1)
            v.tensor_scalar(table[:, MAIN:MAIN + E], next_row[0:1, :], -float(SLOTS), None, ALU.add)
            v.tensor_scalar(row_tmp[:], tile_no[0:1, :], -float(P), None, ALU.mult)
            dve.wait_ge(tb_pe, 3)
            dve.drain()
            v.tensor_copy(table[:, N_OVER:N_OVER + 1], psA[0:1, 4:5])
            v.tensor_scalar(table[:, OV_E:OV_E + OVW], psB[0:1, 0:OVW], float(E - 1), None, ALU.min)
            v.tensor_tensor(row_tmp[:], row_tmp[:], psC[0:1, 0:OVW], ALU.add)
            dve.drain()
            v.tensor_scalar(table[:, OV_ROW:OV_ROW + OVW], row_tmp[:], 0.0, None, ALU.max)
            dve.drain()
            v.tensor_copy(n_row[:], next_row[0:1, :]).then_inc(table_ready, 1)
            dve.wait_ge(table_ready, 1)

            def load(n, q, j, nsub, e, extra_no):
                if e is None:
                    e = dve.value_load(table[0:1, bass.ds(extra_no + OV_E, 1)], min_val=0, max_val=E - 1)
                dve.wait_ge(x_loaded[j], q * 16 + 16)
                v.tensor_copy(pcol[:, j, 0:nsub], xt[:, j, 0:nsub, bass.ds(e + PR, 1)].rearrange("p a o -> p (a o)")
                              ).then_inc(pcol_ready, 1)

            def up(n, q, j, nsub):
                dve.wait_ge(gate_ready, n + 1)
                wait(dve, down_ready, n - 1)
                v.tensor_tensor(hid[:, j % 2, 0:nsub * P], gate[:, j % 2, 0:nsub * P],
                                psG[j % 2][:, SLOTS:SLOTS + nsub * P], ALU.mult).then_inc(hid_ready, 1)

            def down(n, q, j, nsub):
                dve.wait_ge(down_ready, n + 1)
                dve.wait_ge(pcol_ready, n + 1)
                v.tensor_scalar(y[:, j, 0, :], psY[0][j % 2][:, 0:D], pcol[:, j, 0:1], None, ALU.mult).then_inc(y_dve, 1)

            run_phase2(dve, load, up, down)

            for i in range(TT // 4):
                dve.wait_ge(fin_loaded[i % 2], (i // 2 + 1) * 32)
                wait(dve, fin_stored[i % 2], i // 2 * 16)
                v.tensor_tensor(fin_sum[:, i % 2, :, :], fin_a[:, i % 2, :, :], fin_b[:, i % 2, :, :],
                                ALU.add).then_inc(fin_ready, 1)

        @block.tensor
        def _(pe):
            mm, tp = nc.tensor.matmul, nc.tensor.transpose
            pe.wait_ge(ld_const, N_LD_CONST * 16)
            pe.wait_ge(made_consts, 1)
            pe.wait_ge(made_ones, 4)

            def transpose_tiles(ps, source):
                for t in range(NT):
                    for c in range(2):
                        last = tp(ps[:, c * S + t * P:c * S + (t + 1) * P], source[:, t, c * P:(c + 1) * P], ident)
                return last

            def step(i, h, par, s):
                if s < U:
                    u, n, (t, h0, nh, nk) = s, i * U + s, unit_shape(s)
                    if u == 0:
                        pe.wait_ge(qT_ready, i + 1)
                        pe.wait_ge(kbd_ready, i + 1)
                    wait(pe, probs_ready, n - 1)
                    g0 = h0 % G
                    mm(psS[u % 2][:].rearrange("p (h k) -> p h k", h=nh), qT[:, par, h0 // G, t * P:(t + 1) * P],
                       kbd[:, par, g0:g0 + nh, 0:nk], start=True, stop=False)
                    mm(psS[u % 2][:].rearrange("p (h k) -> p h k", h=nh)[:, :, nk - P:nk], ident_bf[:],
                       mask_bf[:, 0:nh, :], start=False, stop=True).then_inc(scores_ready, 1)
                if 1 <= s <= U:
                    u, n = s - 1, i * U + (s - 1)
                    pe.wait_ge(probs_ready, n + 1)
                    wait(pe, (pT_dve, pT_act)[u % 2], i * (U // 2) + u // 2)
                    for k in range(4):
                        last = tp(psT[u % 2][:, k * P:(k + 1) * P], probs[:, u % 2, k * P:(k + 1) * P], ident)
                    last.then_inc(pT_in, 1)
                if s >= 2:
                    u, n, (t, h0, nh, nk) = s - 2, i * U + (s - 2), unit_shape(s - 2)
                    pe.wait_ge((pT_dve, pT_act)[u % 2], i * (U // 2) + (u // 2 + 1))
                    if u == 0:
                        pe.wait_ge(v_ready, i * NT + NT)
                    if u in (0, 4):
                        wait(pe, attn_ready, i * NT + t)
                    for k in range(nh):
                        for kt in range(t + 1):
                            block_no = k * (t + 1) + kt
                            last = mm(psO[:, (h0 + k) * VW:(h0 + k + 1) * VW],
                                      pT[:, u % 2, block_no * P:(block_no + 1) * P], v1[:, par, kt, :],
                                      start=(kt == 0), stop=(kt == t))
                    last.then_inc(pv_done, 1)

            def stage1(i, h, par, piece):
                if piece == 1:
                    pe.wait_ge(xn_ready, i + 1)
                    wait(pe, qT_ready, i)
                    transpose_tiles(psA, xn).then_inc(xnT_in, 1)
                if piece == 2:
                    pe.wait_ge(xnT_ready, i + 1)
                    wait(pe, kbd_ready, i)
                    for t in range(NT):
                        for c in range(2):
                            last = mm((psB, psA)[t][:, 0:QKV], xnT[:, c, t * P:(t + 1) * P], wqkv_sb[:, c, :],
                                      start=(c == 0), stop=(c == 1))
                        last.then_inc(qkv_ready, 1)
                if piece == 3:
                    pe.wait_ge(qk_ready, i * NT + NT)
                    pe.wait_ge(v_ready, i * NT + NT)
                    transpose_tiles(psA, qk)
                    for t in range(NT):
                        last = tp(psB[:, t * P:(t + 1) * P], krep[:, t, :, :].rearrange("p g w -> p (g w)"), ident)
                    last.then_inc(qkT_in, 1)

            def stage3(i, h, par, piece):
                if piece == 0:
                    pe.wait_ge(attn_ready, i * NT + NT)
                    wait(pe, slots_ready, i)
                    transpose_tiles(psC, attn).then_inc(attnT_in, 1)
                if piece == 1:
                    pe.wait_ge(attnT_ready, i + 1)
                    for t in range(NT):
                        for c in range(2):
                            last = mm(psC[:, t * D:(t + 1) * D], attnT[:, c, t * P:(t + 1) * P], wproj_sb[:, c, :],
                                      start=(c == 0), stop=(c == 1))
                    last.then_inc(proj_ready, 1)
                if piece == 2:
                    pe.wait_ge(xn2_ready, i + 1)
                    transpose_tiles(psC, row_sb[:, par, :, :]).then_inc(xn2T_in, 1)
                if piece == 3:
                    pe.wait_ge(xn2T_ready, i + 1)
                    for t in range(NT):
                        for c in range(2):
                            last = mm(psC[:, t * E:(t + 1) * E], xn2T[:, c, t * P:(t + 1) * P], wrouter_sb[:, c, :],
                                      start=(c == 0), stop=(c == 1))
                    last.then_inc(logits_ready, 1)
                if piece == 4:
                    pe.wait_ge(chosen_ready, i + 1)
                    for t in range(NT):
                        c0 = (1 + t) * 2 * E
                        mm(psC[:, c0:c0 + E], tri[:], chosen[:, t, :], start=True, stop=True)
                        last = mm(psC[:, c0 + E:c0 + 2 * E], ones_bf[:], chosen[:, t, :], start=True, stop=True)
                    last.then_inc(rank_ready, 1)

            run_phase1(pe, step, stage1, stage3)

            pe.wait_ge(tb_dve, 1)
            mm(psA[0:E, 0:1], n_row[:], ones[0:1, :], start=True, stop=True).then_inc(tb_pe, 1)
            pe.wait_ge(tb_dve, 2)
            mm(psA[0:E, 2:3], tri_f[0:E, 0:E], over[:], start=True, stop=True).then_inc(tb_pe, 1)
            pe.wait_ge(tb_dve, 3)
            mm(psA[0:1, 4:5], ones[0:E, :], over[:], start=True, stop=True)
            mm(psB[0:1, 0:OVW], ones[0:E, :], ended[:], start=True, stop=True)
            mm(psC[0:1, 0:OVW], over_base[:], begun[:], start=True, stop=True).then_inc(tb_pe, 1)
            pe.wait_ge(table_ready, 1)

            def load(n, q, j, nsub, e, extra_no):
                pe.wait_ge(x_loaded[j], q * 16 + 16)
                wait(pe, xtT_ready, n - 1)
                for a in range(nsub):
                    for c in range(2):
                        last = tp(psX[j % 2][:, c * S + a * P:c * S + (a + 1) * P], xt[:, j, a, c * P:(c + 1) * P], ident)
                last.then_inc(xtT_in, 1)

            def up(n, q, j, nsub):
                pe.wait_ge(w_loaded[j], q * 16 + 16)
                pe.wait_ge(xtT_ready, n + 1)
                wait(pe, hid_ready, n - 1)
                for gu in range(2):
                    for c in range(2):
                        last = mm(psG[j % 2][:, gu * SLOTS:gu * SLOTS + nsub * P],
                                  w_sb[:, j, c * 2 * F + gu * F:c * 2 * F + (gu + 1) * F],
                                  xtT[:, j % 2, c, 0:nsub * P], start=(c == 0), stop=(c == 1))
                last.then_inc(gu_ready, 1)

            def down(n, q, j, nsub):
                pe.wait_ge(hid_ready, n + 1)
                wait(pe, y_dve, n - 1)
                wait(pe, y_act, n - 1 if nsub == NT else E)
                for a in range(nsub):
                    last = mm(psY[a][j % 2][:, 0:D], hid[:, j % 2, a * P:(a + 1) * P],
                              w_sb[:, j, 4 * F:4 * F + D], start=True, stop=True)
                last.then_inc(down_ready, 1)

            run_phase2(pe, load, up, down)


def tables():
    import numpy as np

    f32 = np.float32
    inv_freq = (f32(1.0) / f32(10000.0) ** (np.arange(0, HD, 2, dtype=f32) / f32(HD))).astype(f32)
    t = np.arange(S, dtype=f32)
    freqs = np.einsum("i,j->ij", t, inv_freq).astype(f32)
    freqs = np.concatenate((freqs, freqs), axis=-1)
    base = ((np.arange(0, HD, 2, dtype=f32) + f32(0.4 * HD)) / f32(1.4 * HD)).astype(f32)
    power = ((t - S // 2) / 64).astype(f32)
    scale = (base[None, :] ** power[:, None]).astype(f32)
    scale = np.concatenate((scale, scale), axis=-1)
    sign = np.concatenate((-np.ones(HD // 2), np.ones(HD // 2))).astype(f32)
    weight = f32(HD ** -0.5)
    inverse = (f32(1.0) / scale).astype(f32)
    cos = np.concatenate([np.tile(np.cos(freqs) * scale, (1, H)), np.cos(freqs) * inverse], axis=1) * weight
    sin = np.concatenate([np.tile(np.sin(freqs) * scale * sign, (1, H)), np.sin(freqs) * inverse * sign], axis=1) * weight
    p = np.arange(P)
    consts = np.concatenate([
        np.eye(P), p[:, None] < p[None, :], np.where(p[None, :] > p[:, None], MASKED, 0.0),
        p[:, None] // HD == np.arange(G)[None, :],
        np.broadcast_to(np.arange(E) * REGION + PAD, (P, E)),
        (np.minimum(p, E - 1) * REGION + PAD)[:, None],
        p[:, None] + P * np.arange(NT)[None, :],
    ], axis=1)
    return cos.astype(f32), sin.astype(f32), consts.astype(f32)


def kernel(L0_attn_hidden_states, L0_attn_w_q, L0_attn_w_kv, L0_attn_w_proj, L0_attn_b_proj,
           L0_ffn_router_weight, L0_ffn_gate_up_proj, L0_ffn_down_proj):
    import numpy as np
    import concourse.bacc as bacc
    from concourse.bass_utils import run_bass_kernel_spmd as run

    a = np.asarray
    c = np.ascontiguousarray
    gu = a(L0_ffn_gate_up_proj).transpose(0, 2, 1).reshape(E, 2, P, 2 * F).transpose(0, 2, 1, 3).reshape(E, P, 4 * F)
    dn = a(L0_ffn_down_proj).transpose(0, 2, 1)
    cos, sin, consts = tables()
    arrays = {
        "x": c(a(L0_attn_hidden_states).reshape(T, D)),
        "wqkv": c(np.concatenate([a(L0_attn_w_q).T, a(L0_attn_w_kv).T], axis=1)),
        "wproj": c(a(L0_attn_w_proj).T),
        "bproj": c(a(L0_attn_b_proj)),
        "wrouter": c(a(L0_ffn_router_weight).T),
        "wexpert": c(np.concatenate([gu, dn], axis=2).reshape(E * P, WCOLS)),
        "cos": cos, "sin": sin, "consts": consts,
    }
    nc = bacc.Bacc("TRN2", target_bir_lowering=False, num_devices=1)
    args = [nc.dram_tensor(n, v.shape, F32, kind="ExternalInput").ap() for n, v in arrays.items()]
    out = nc.dram_tensor("out_0_dram", (T, D), F32, kind="ExternalOutput").ap()
    rows = nc.dram_tensor("rows", (E * REGION, ROW), F32, kind="Internal").ap()
    acc = [nc.dram_tensor(f"acc{i}", (T + PAD, D), F32, kind="Internal").ap() for i in range(2)]
    moe_block(nc, *args, out, rows, *acc)
    r = run(nc, [arrays], core_ids=[0])
    return r.results[0]["out_0_dram"].reshape(B, S, D)
```

```python
from contextlib import ExitStack

import concourse.bass as bass
from concourse import mybir
from concourse.alu_op_type import AluOpType as ALU

ACT = mybir.ActivationFunctionType
AX = mybir.AxisListType
F32 = mybir.dt.float32
BF16 = mybir.dt.bfloat16
I32 = mybir.dt.int32
U32 = mybir.dt.uint32

P = 128
B, S, D = 8, 256, 256
T = B * S
NT = S // P
H, HD = 16, 16
G = P // HD
QK = H * HD + HD
QKV = QK + HD
E, TOPK, F = 64, 8, 128
EPS = 1e-5
MASKED = -3.0e38
RSQRT_SEED = float(0x5F3759DF)

U = 12
VW = HD + 1

SLOTS = NT * P
PAD = SLOTS
REGION = PAD + T
ID, PR = D, D + 1
ROW = D + 1 + E
WCOLS = 2 * 2 * F + D
OVER = max(min(k * ((T - SLOTS) // P), (T * TOPK - k * SLOTS + k * (P - 1)) // P) for k in range(1, E + 1))
NB = 8
ACC_OF = (0, 1, 2, 0, 1, 2, 1, 2)
LAST_ADD = [next(k for k in range(1, NB + 1) if ACC_OF[(j - k) % NB] == a) for j, a in enumerate(ACC_OF)]
WARM_START, WARM_ROTARY, WARM_STEP, WARM_ROOT, WARM_UNITS = 22, 10, 3, 24, 38
AHEAD = 4
SP_LOADS = (0, 4)
SKIP = 4
GROUPS = -(-(OVER + 2 - NB) // (NB * SKIP))
OVW = NB + GROUPS * SKIP * NB + AHEAD


def unit_shape(u):
    return (0, 4 * u, 4, P) if u < 4 else (1, 2 * (u - 4), 2, S)


def wait(eng, sem, value):
    if isinstance(value, int) and value <= 0:
        return
    eng.wait_ge(sem, value)


def moe_block(nc, x, wqkv, wproj, bproj, wrouter, wexpert, cos_t, sin_t, consts, out, rows, acc1, acc2):
    acc = (out, acc1, acc2)
    with ExitStack() as ctx:
        def sb(name, shape, dt=F32):
            return ctx.enter_context(nc.sbuf_tensor(name, shape, dt))

        def sem(name):
            return ctx.enter_context(nc.semaphore(name))

        tri = sb("tri", [P, P], BF16)
        ident_bf = sb("ident_bf", [P, P], BF16)
        mask_bf = sb("mask_bf", [P, 4, P], BF16)
        ones_bf = sb("ones_bf", [P, P], BF16)
        ones = sb("ones", [P, 1])
        unused = sb("unused", [P, 1])
        consts_sb = sb("consts_sb", [P, 3 * P + G + E + 1 + NT])
        ident, tri_f, mask_f = (consts_sb[:, k * P:(k + 1) * P] for k in range(3))
        head_mask = consts_sb[:, 3 * P:3 * P + G]
        region_row = consts_sb[:, 3 * P + G:3 * P + G + E]
        region_col = consts_sb[:, 3 * P + G + E:3 * P + G + E + 1]
        token0 = consts_sb[:, 3 * P + G + E + 1:3 * P + G + E + 1 + NT]
        wqkv_sb = sb("wqkv_sb", [P, 2, QKV])
        wproj_sb = sb("wproj_sb", [P, 2, D])
        wrouter_sb = sb("wrouter_sb", [P, 2, E])
        bias_sb = sb("bias_sb", [P, D])
        cos_sb = sb("cos_sb", [P, NT, QK])
        sin_sb = sb("sin_sb", [P, NT, QK])
        x_sb = sb("x_sb", [P, 2, NT, D])
        stats = sb("stats", [P, 2 * NT, 6])
        mv = sb("mv", [P, 2 * NT, 2])
        var = sb("var", [P, 2 * NT])
        rstd = sb("rstd", [P, 2 * NT])
        shift = sb("shift", [P, 2 * NT])
        guess = sb("guess", [P, 2 * NT])
        xn = sb("xn", [P, 2, NT, D])
        xnT = sb("xnT", [P, 2, S])
        rot_a = sb("rot_a", [P, NT, QK])
        rot_b = sb("rot_b", [P, NT, QK])
        qk = sb("qk", [P, NT, QK])
        krep = sb("krep", [P, NT, G, HD])
        qT = sb("qT", [P, 2, 2, S])
        kbd = sb("kbd", [P, 2, G, S])
        v1 = sb("v1", [P, 2, NT, VW])
        neg_max = sb("neg_max", [P, 2, 4])
        probs = sb("probs", [P, 2, 512])
        pT = sb("pT", [P, 2, 512])
        rden = sb("rden", [P, H])
        attn = sb("attn", [P, NT, D])
        attnT = sb("attnT", [P, 2, S])
        xb = sb("xb", [P, 2, NT, D])
        x2 = sb("x2", [P, 2, NT, D])
        token = sb("token", [P, NT])
        row_sb = sb("row_sb", [P, 2, NT, ROW])
        xn2T = sb("xn2T", [P, 2, S])
        neg_top = sb("neg_top", [P, NT])
        esum = sb("esum", [P, NT])
        eprob = sb("eprob", [P, NT, E])
        top8 = sb("top8", [P, NT, TOPK])
        marked = sb("marked", [P, NT, E])
        chosen = sb("chosen", [P, NT, E], BF16)
        next_row = sb("next_row", [P, E])
        slot = sb("slot", [P, NT, E])
        slot8 = sb("slot8", [P, NT, TOPK])
        slot_ix = sb("slot_ix", [P, 2, NT, TOPK], U32)
        zeros = sb("zeros", [P, 2, ROW])
        n_row = sb("n_row", [1, E])
        over_i = sb("over_i", [E, 1], I32)
        over = sb("over", [E, 1])
        over_end = sb("over_end", [E, 1])
        over_start = sb("over_start", [E, 1])
        over_base = sb("over_base", [E, 1])
        tile_no = sb("tile_no", [E, OVW])
        ended = sb("ended", [E, OVW])
        begun = sb("begun", [E, OVW])
        table = sb("table", [1, 1 + E + 2 * OVW], I32)
        row_tmp = sb("row_tmp", [1, OVW])
        N_OVER, MAIN, OV_E, OV_ROW = 0, 1, 1 + E, 1 + E + OVW
        w_sb = sb("w_sb", [P, NB, WCOLS])
        xt = sb("xt", [P, NB, NT, ROW])
        xtT = sb("xtT", [P, 2, 2, SLOTS])
        pcol = sb("pcol", [P, NB, NT])
        gate = sb("gate", [P, 2, SLOTS])
        hid = sb("hid", [P, 2, SLOTS])
        y = sb("y", [P, NB, NT, D])

        psA = ctx.enter_context(nc.psum_tensor("psA", [P, 512], F32))
        psB = ctx.enter_context(nc.psum_tensor("psB", [P, 512], F32))
        psC = ctx.enter_context(nc.psum_tensor("psC", [P, 512], F32))
        psO = ctx.enter_context(nc.psum_tensor("psO", [P, 512], F32))
        psS = [ctx.enter_context(nc.psum_tensor(f"psS{i}", [P, 512], F32)) for i in range(2)]
        psT = [ctx.enter_context(nc.psum_tensor(f"psT{i}", [P, 512], F32)) for i in range(2)]
        psX, psG, psY = [psA, psB], psS, [psT, [psC, psO]]

        ld_consts, ld_qkv, ld_rotary, ld_rest = (sem(n) for n in ("ld_consts", "ld_qkv", "ld_rotary", "ld_rest"))
        ld_x = [sem(f"ld_x{i}") for i in range(2)]
        ld_xb = [sem(f"ld_xb{i}") for i in range(2)]
        root_ready = sem("root_ready")
        made_ones = sem("made_ones")
        made_consts = sem("made_consts")
        made_zero = sem("made_zero")
        zero_stored = sem("zero_stored")
        xn_ready, xnT_in, xnT_ready, qkv_ready = (sem(n) for n in ("xn_ready", "xnT_in", "xnT_ready", "qkv_ready"))
        v_ready, rot_ready, qk_ready = (sem(n) for n in ("v_ready", "rot_ready", "qk_ready"))
        qkT_in, qT_ready, kbd_ready, xb_ready = (sem(n) for n in ("qkT_in", "qT_ready", "kbd_ready", "xb_ready"))
        scores_ready, max_ready, probs_ready = (sem(n) for n in ("scores_ready", "max_ready", "probs_ready"))
        pT_in, pT_act, pT_dve, pv_done = (sem(n) for n in ("pT_in", "pT_act", "pT_dve", "pv_done"))
        attn_ready = sem("attn_ready")
        attnT_in, attnT_ready, proj_ready, x2_ready = (sem(n) for n in ("attnT_in", "attnT_ready", "proj_ready", "x2_ready"))
        x2_stored = [sem(f"x2_stored{i}") for i in range(2)]
        xn2_ready, xn2T_in, xn2T_ready, logits_ready = (sem(n) for n in ("xn2_ready", "xn2T_in", "xn2T_ready", "logits_ready"))
        top_ready, exp_ready, chosen_ready = (sem(n) for n in ("top_ready", "exp_ready", "chosen_ready"))
        rank_ready, slots_ready = sem("rank_ready"), sem("slots_ready")
        row_free = sem("row_free")
        sent = [[sem(f"sent{p}{t}") for t in range(NT)] for p in range(2)]
        pool_go = sem("pool_go")
        tb_dve, tb_pe, table_ready = sem("tb_dve"), sem("tb_pe"), sem("table_ready")
        w_loaded = [sem(f"w_loaded{j}") for j in range(NB)]
        x_loaded = [sem(f"x_loaded{j}") for j in range(NB)]
        xtT_in, xtT_ready, pcol_ready = sem("xtT_in"), sem("xtT_ready"), sem("pcol_ready")
        gu_ready, gate_ready, hid_ready, down_ready = (sem(n) for n in ("gu_ready", "gate_ready", "hid_ready", "down_ready"))
        y_dve, y_act = sem("y_dve"), sem("y_act")
        added = [sem(f"added{j}") for j in range(NB)]
        summed = [sem(f"summed{half}") for half in range(2)]

        block = ctx.enter_context(nc.Block())


        def after(i, h, par):
            return (i + 1, h + 1, 0) if par else (i + 1, h, 1)

        def before(i, h, par):
            return (i - 1, h, 0) if par else (i - 1, h - 1, 1)

        def nothing(*_):
            pass

        def run_phase1(eng, score=nothing, turn=nothing, weigh=nothing, stage3=nothing, stage1=nothing,
                       ahead=nothing, root=nothing):
            def batch(b, first=False, last=False, end=False):
                for s in range(U):
                    score(*b, s)
                    if s >= 1:
                        turn(*b, s - 1)
                    elif not first:
                        turn(*before(*b), U - 1)
                    if s >= 2:
                        weigh(*b, s - 2)
                    elif not first:
                        weigh(*before(*b), s - 2 + U)
                    if not first:
                        stage3(*before(*b), s)
                    if not last:
                        stage1(*after(*b), s)
                    if not end:
                        ahead(*after(*after(*b)), s)
                    root(*b, s)

            ahead(0, 0, 0, -1)
            ahead(1, 0, 1, -1)
            root(-1, None, None, -1)
            ahead(0, 0, 0, -2)
            ahead(1, 0, 1, -2)
            for s in range(U):
                stage1(0, 0, 0, s)
            batch((0, 0, 0), first=True)
            batch((1, 0, 1))
            with eng.Fori(1, (B - 2) // 2) as it:
                batch((it * 2, it, 0))
                batch((it * 2 + 1, it, 1))
            batch((B - 2, B // 2 - 1, 0), end=True)
            batch((B - 1, B // 2 - 1, 1), end=True, last=True)
            b = (B - 1, B // 2 - 1, 1)
            turn(*b, U - 1)
            weigh(*b, U - 2)
            weigh(*b, U - 1)
            for s in range(U):
                stage3(*b, s)
                root(B, None, None, s)

        def run_phase2(eng, load=nothing, up=nothing, down=nothing):
            n_over = eng.value_load(table[0:1, N_OVER:N_OVER + 1], min_val=0, max_val=OVER)

            def main(m, q, j):
                if not isinstance(m, int) or m < E:
                    load(m, q, j, NT, m, None, n_over)
                if not isinstance(m, int) or 1 <= m <= E:
                    up(m - 1, q if j >= 1 else q - 1, (j - 1) % NB, NT)
                if not isinstance(m, int) or 2 <= m:
                    down(m - 2, q if j >= 2 else q - 1, (j - 2) % NB, NT)

            for m in range(NB):
                main(m, 0, m)
            with eng.Fori(1, E // NB) as q:
                for j in range(NB):
                    main(q * NB + j, q, j)
            for m in range(E, E + 2):
                main(m, m // NB, m % NB)

            def extra(m, q, j):
                if load is not nothing and (not isinstance(m, int) or m < OVER):
                    with eng.If(n_over > m):
                        load(m + E, q + E // NB, j, 1, None, m, n_over)
                if up is not nothing and (not isinstance(m, int) or m >= 1):
                    with eng.If(n_over > m - 1):
                        up(m + (E - 1), (q if j >= 1 else q - 1) + E // NB, (j - 1) % NB, 1)
                if down is not nothing and (not isinstance(m, int) or m >= 2):
                    with eng.If(n_over > m - 2):
                        down(m + (E - 2), (q if j >= 2 else q - 1) + E // NB, (j - 2) % NB, 1)

            for m in range(NB):
                extra(m, 0, m)
            with eng.Fori(0, GROUPS) as group:
                with eng.If(n_over > group * (SKIP * NB) + (NB - 2)):
                    with eng.Fori(0, SKIP) as k:
                        q = group * SKIP + k + 1
                        with eng.If(n_over > q * NB - 2):
                            for j in range(NB):
                                extra(q * NB + j, q, j)

        def adds_before(q, j, nsub):
            return q * (16 * NT) if nsub == NT else (q - E // NB) * 16 + E // NB * 16 * NT

        def rows_of(dram, r0, n):
            return dram[bass.ds(r0, n * P), :].rearrange("(a p) n -> p a n", p=P)

        def load_weights(eng, e, j):
            eng.dma_start(w_sb[:, j, :], wexpert[bass.ds(e * P, P), :]).then_inc(w_loaded[j], 16)

        @block.sync
        def _(sp):
            for par in range(2):
                sp.sem_inc(x2_stored[par], 16)
            sp.sem_inc(row_free, 1)

            def load_x(i, h, par):
                wait(sp, xn_ready, i - 1)
                sp.dma_start(x_sb[:, par, :, :], rows_of(x, i * S, NT)).then_inc(ld_x[par], 16)

            load_x(0, 0, 0)
            sp.dma_start(consts_sb[:], consts[:, :]).then_inc(ld_consts, 16)
            load_x(1, 0, 1)
            sp.dma_start(wqkv_sb[:], wqkv.rearrange("(c p) n -> p c n", p=P)).then_inc(ld_qkv, 16)
            sp.dma_start(cos_sb[:], cos_t.rearrange("(a p) n -> p a n", p=P)).then_inc(ld_rotary, 16)
            sp.dma_start(sin_sb[:], sin_t.rearrange("(a p) n -> p a n", p=P)).then_inc(ld_rotary, 16)
            sp.dma_start(bias_sb[:], bproj.partition_broadcast(P)).then_inc(ld_rest, 16)
            sp.dma_start(wproj_sb[:], wproj.rearrange("(c p) n -> p c n", p=P)).then_inc(ld_rest, 16)
            sp.dma_start(wrouter_sb[:], wrouter.rearrange("(c p) n -> p c n", p=P)).then_inc(ld_rest, 16)

            sp.wait_ge(made_zero, 1 + NT)
            for a in range((T + PAD) // PAD):
                for k in (1, 2):
                    sp.dma_start(rows_of(acc[k], a * PAD, NT), zeros[:, :, 0:D]).then_inc(zero_stored, 16)
            sp.dma_start(rows_of(acc[0], T, NT), zeros[:, :, 0:D]).then_inc(zero_stored, 16)

            def stage3(i, h, par, s):
                if s == 4:
                    sp.wait_ge(x2_ready, i + 1)
                    sp.dma_start(rows_of(acc[0], i * S, NT), x2[:, par, :, :]).then_inc(x2_stored[par], 16)

                if s == 10 and not (isinstance(i, int) and i == 0):
                    _, h_before, par_before = before(i, h, par)
                    for t in range(NT):
                        sp.wait_ge(sent[par_before][t], (h_before + 1) * (TOPK * 16))
                    sp.sem_inc(row_free, 1)

            def ahead(i, h, par, s):
                if s == 0:
                    load_x(i, h, par)

            def root(i, h, par, s):
                if s == 5 and h is not None:
                    wait(sp, x2_ready, i - 1)
                    sp.dma_start(xb[:, par, :, :], rows_of(x, i * S, NT)).then_inc(ld_xb[par], 16)
                if 0 <= s < E // B and h is not None:
                    sp.dma_start(rows_of(rows, (i * (E // B) + s) * REGION, NT), zeros[:]).then_inc(zero_stored, 16)

            run_phase1(sp, stage3=stage3, ahead=ahead, root=root)

            for e in range(NB):
                load_weights(sp, e, e)
            sp.wait_ge(table_ready, 1)

            def load(n, q, j, nsub, e, extra_no, n_over):
                own_weights = not (isinstance(n, int) and n < NB)
                if e is None:
                    own_weights = j in SP_LOADS or isinstance(n, int) and n < E + AHEAD
                if e is None and own_weights:
                    e = sp.value_load(table[0:1, bass.ds(extra_no + OV_E, 1)], min_val=0, max_val=E - 1)
                if extra_no is not None:
                    r0 = sp.value_load(table[0:1, bass.ds(extra_no + OV_ROW, 1)], min_val=0,
                                       max_val=E * REGION - P)
                else:
                    r0 = sp.value_load(table[0:1, bass.ds(e + MAIN, 1)], min_val=0,
                                       max_val=E * REGION - SLOTS)
                if isinstance(n, int) and n == 0:
                    for p in range(2):
                        for t in range(NT):
                            sp.wait_ge(sent[p][t], B // 2 * TOPK * 16)
                    sp.wait_ge(zero_stored, (2 * ((T + PAD) // PAD) + 1 + E) * 16)
                wait(sp, added[j], adds_before(q, j, nsub))
                sp.dma_start(xt[:, j, 0:nsub, :], rows_of(rows, r0, nsub)).then_inc(x_loaded[j], 16)
                if own_weights:
                    wait(sp, down_ready, n - (NB - 1))
                    load_weights(sp, e, j)

            run_phase2(sp, load=load)

        @block.gpsimd
        def _(pool):
            nc.gpsimd.memset(zeros[:], 0.0).then_inc(made_zero, 1)
            nc.gpsimd.memset(v1[:], 1.0).then_inc(made_ones, 1)
            nc.gpsimd.memset(ones[:], 1.0).then_inc(made_ones, 1)
            nc.gpsimd.memset(ones_bf[:], 1.0).then_inc(made_ones, 1)
            nc.gpsimd.iota(tile_no[:], [[1, OVW]], base=0, channel_multiplier=0,
                           allow_small_or_imprecise_dtypes=True).then_inc(made_ones, 1)
            pool.wait_ge(made_zero, 1)
            for a in range(NT):
                nc.gpsimd.iota(zeros[:, a, ID:ID + 1].bitcast(I32), [[0, 1]], base=T + a * P,
                               channel_multiplier=1).then_inc(made_zero, 1)


            def stage1(i, h, par, s):
                if s == 7:
                    wait(pool, qkT_in, i)
                    for t in range(NT):
                        pool.wait_ge(rot_ready, i * NT + (t + 1))
                        nc.gpsimd.tensor_tensor(qk[:, t, :], rot_a[:, t, :], rot_b[:, t, :], ALU.add)
                        key_a, key_b = (r[:, t, H * HD:QK].unsqueeze(1).to_broadcast([P, G, HD])
                                        for r in (rot_a, rot_b))
                        nc.gpsimd.tensor_tensor(krep[:, t, :, :], key_a, key_b, ALU.add).then_inc(qk_ready, 1)

            def root(i, h, par, s):
                if s == 8 and h is not None:
                    pool.wait_ge(ld_rest, 3 * 16)
                    pool.wait_ge(ld_xb[par], h * 16 + 16)
                    nc.gpsimd.tensor_tensor(xb[:, par, :, :], xb[:, par, :, :],
                                            bias_sb[:].unsqueeze(1).to_broadcast([P, NT, D]),
                                            ALU.add).then_inc(xb_ready, 1)

            def stage3(i, h, par, s):
                if s == 11:
                    pool.wait_ge(slots_ready, i + 1)
                    pool.sem_inc(pool_go, 1)
                    for t in range(NT):
                        for k in range(TOPK):
                            nc.gpsimd.indirect_dma_start(
                                rows, bass.IndirectOffsetOnAxis(ap=slot_ix[:, par, t, k:k + 1], axis=0),
                                row_sb[:, par, t, :], None).then_inc(sent[par][t], 16)

            run_phase1(pool, stage1=stage1, stage3=stage3, root=root)
            pool.wait_ge(table_ready, 1)
            for par in range(2):
                pool.wait_ge(x2_stored[par], B // 2 * 16 + 16)
            pool.wait_ge(zero_stored, (2 * ((T + PAD) // PAD) + 1 + E) * 16)

            def down(n, q, j, nsub):
                pool.wait_ge(y_dve, n + 1)
                if nsub == NT:
                    pool.wait_ge(y_act, n + 1)
                back = LAST_ADD[j]
                wait(pool, added[(j - back) % NB], adds_before(q + 1 if j >= back else q, j, nsub))
                pool.sem_inc(pool_go, 1)
                for a in range(nsub):
                    nc.gpsimd.indirect_dma_start(
                        acc[ACC_OF[j]], bass.IndirectOffsetOnAxis(ap=xt[:, j, a, ID:ID + 1].bitcast(U32), axis=0),
                        y[:, j, a, :], None, compute_op=ALU.add).then_inc(added[j], 16)

            run_phase2(pool, down=down)
            n_over = pool.value_load(table[0:1, N_OVER:N_OVER + 1], min_val=0, max_val=OVER)
            for j in range(NB):
                pool.wait_ge(added[j], (n_over + (NB - 1 - j)) // NB * 16 + E // NB * 16 * NT)
            pool.sem_inc(pool_go, 1)
            for a in (1, 2):
                for half in range(2):
                    tokens = slice(half * T // 2, (half + 1) * T // 2)
                    if a == 2:
                        pool.wait_ge(summed[half], 16)
                    pool.dma_start(out[tokens, :], acc[a][tokens, :], accum_op=ALU.add,
                                   max_dma_last_dim=8192).then_inc(summed[half], 16)
            for half in range(2):
                pool.wait_ge(summed[half], 2 * 16)

        @block.scalar
        def _(act):
            act.wait_ge(made_ones, 4)
            nc.scalar.activation(unused[:], ones[:], ACT.Exp)
            act.wait_ge(ld_consts, 16)

            def score(i, h, par, u):
                n, (t, h0, nh, nk) = i * U + u, unit_shape(u)
                act.wait_ge(max_ready, n + 1)
                wait(act, pT_in, n - 1)
                for k in range(nh):
                    last = nc.scalar.activation(probs[:, u % 2, k * nk:(k + 1) * nk],
                                                psS[u % 2][:, k * nk:(k + 1) * nk], ACT.Exp,
                                                bias=neg_max[:, u % 2, k:k + 1])
                last.then_inc(probs_ready, 1)

            def turn(i, h, par, u):
                if u % 2 == 1:
                    n = i * U + u
                    act.wait_ge(pT_in, n + 1)
                    wait(act, pv_done, n - 1)
                    nc.scalar.copy(pT[:, 1, :], psT[1][:]).then_inc(pT_act, 1)

            def normalise(source, result, c0, signal):
                for t in range(NT):
                    last = nc.scalar.activation(result[:, t, 0:D], source[:, t, :], ACT.Identity,
                                                bias=shift[:, c0 + t:c0 + t + 1], scale=rstd[:, c0 + t:c0 + t + 1])
                last.then_inc(signal, 1)

            def ahead(i, h, par, s):
                if s == -2:
                    act.wait_ge(root_ready, 1)
                    normalise(x_sb[:, par, :, :], xn[:, par, :, :], i * NT, xn_ready)
                if s == 7:
                    act.wait_ge(root_ready, i)
                    wait(act, xnT_in, i - 1)
                    normalise(x_sb[:, par, :, :], xn[:, par, :, :], NT, xn_ready)

            def stage1(i, h, par, s):
                if s == 0:
                    act.wait_ge(xnT_in, i + 1)
                    wait(act, qkv_ready, i * NT)
                    nc.scalar.copy(xnT[:].rearrange("p c n -> p (c n)"), psA[:]).then_inc(xnT_ready, 1)
                if s == 9:
                    act.wait_ge(qkT_in, i + 1)
                    wait(act, scores_ready, (i - 1) * U)
                    nc.scalar.copy(qT[:, par, :, :].rearrange("p c n -> p (c n)"), psA[:]).then_inc(qT_ready, 1)
                if s in (9, 10):
                    for g in range((s - 9) * G // 2, (s - 8) * G // 2):
                        last = nc.scalar.mul(kbd[:, par, g, :], psB[:, 0:S], head_mask[:, g:g + 1])
                    last.then_inc(kbd_ready, 1)

            def stage3(i, h, par, s):
                if s == 2:
                    act.wait_ge(attnT_in, i + 1)
                    wait(act, proj_ready, i)
                    nc.scalar.copy(attnT[:].rearrange("p c n -> p (c n)"), psC[:]).then_inc(attnT_ready, 1)
                if s == 6:
                    act.wait_ge(root_ready, i + 3)
                    wait(act, row_free, i)
                    normalise(x2[:, par, :, :], row_sb[:, par, :, :], 0, xn2_ready)
                if s == 7:
                    act.wait_ge(xn2T_in, i + 1)
                    wait(act, logits_ready, i)
                    nc.scalar.copy(xn2T[:].rearrange("p c n -> p (c n)"), psC[:]).then_inc(xn2T_ready, 1)
                if s == 8:
                    act.wait_ge(top_ready, i + 1)
                    for t in range(NT):
                        last = nc.scalar.activation(eprob[:, t, :], psC[:, t * E:(t + 1) * E], ACT.Exp,
                                                    bias=neg_top[:, t:t + 1], accum_out=esum[:, t:t + 1])
                    last.then_inc(exp_ready, 1)

            run_phase1(act, score, turn, stage3=stage3, stage1=stage1, ahead=ahead)
            nc.scalar.activation(unused[:], ones[:], ACT.Silu)
            act.wait_ge(table_ready, 1)

            def load(n, q, j, nsub, e, extra_no, n_over):
                act.wait_ge(xtT_in, n + 1)
                wait(act, gu_ready, n - 1)
                nc.scalar.copy(xtT[:, j % 2, :, 0:nsub * P],
                               psX[j % 2][:].rearrange("p (c n) -> p c n", c=2)[:, :, 0:nsub * P]
                               ).then_inc(xtT_ready, 1)
                ahead_j = (j + AHEAD) % NB
                if extra_no is not None and ahead_j not in SP_LOADS:
                    with act.If(n_over > extra_no + AHEAD):
                        e = act.value_load(table[0:1, bass.ds(extra_no + (OV_E + AHEAD), 1)], min_val=0,
                                           max_val=E - 1)
                        wait(act, down_ready, n + (AHEAD - NB + 1))
                        load_weights(act, e, ahead_j)

            def up(n, q, j, nsub):
                act.wait_ge(gu_ready, n + 1)
                wait(act, hid_ready, n - 1)
                nc.scalar.activation(gate[:, j % 2, 0:nsub * P], psG[j % 2][:, 0:nsub * P],
                                     ACT.Silu).then_inc(gate_ready, 1)

            def down(n, q, j, nsub):
                if nsub == NT:
                    act.wait_ge(down_ready, n + 1)
                    act.wait_ge(pcol_ready, n + 1)
                    nc.scalar.mul(y[:, j, 1, :], psY[1][j % 2][:, 0:D], pcol[:, j, 1:2]).then_inc(y_act, 1)

            run_phase2(act, load, up, down)

        @block.vector
        def _(dve):
            v = nc.vector

            dve.wait_ge(ld_consts, 16)
            dve.wait_ge(made_ones, 4)
            v.tensor_copy(tri[:], tri_f)
            v.tensor_copy(ident_bf[:], ident)
            v.tensor_copy(mask_bf[:], mask_f.unsqueeze(1).to_broadcast([P, 4, P]))
            v.tensor_copy(token[:], token0)
            v.tensor_copy(next_row[:], region_row).then_inc(made_consts, 1)

            def score(i, h, par, u):
                n, (t, h0, nh, nk) = i * U + u, unit_shape(u)
                dve.wait_ge(scores_ready, n + 1)
                wait(dve, probs_ready, n - 1)
                v.reduce_max(neg_max[:, u % 2, 0:nh], psS[u % 2][:].rearrange("p (h k) -> p h k", h=nh),
                             AX.X, negate=True).then_inc(max_ready, 1)

            def turn(i, h, par, u):
                if u % 2 == 0:
                    n = i * U + u
                    dve.wait_ge(pT_in, n + 1)
                    wait(dve, pv_done, n - 1)
                    v.tensor_copy(pT[:, 0, :], psT[0][:]).then_inc(pT_dve, 1)

            def weigh(i, h, par, u):
                if u in (3, U - 1):
                    t = 0 if u == 3 else 1
                    dve.wait_ge(pv_done, i * U + (u + 1))
                    wait(dve, attnT_in, i)
                    heads = psO[:, 0:H * VW].rearrange("p (h w) -> p h w", w=VW)
                    v.reciprocal(rden[:].unsqueeze(2), heads[:, :, HD:VW])
                    dve.drain()
                    v.tensor_tensor(attn[:, t, :].rearrange("p (h w) -> p h w", w=HD), heads[:, :, 0:HD],
                                    rden[:].unsqueeze(2).to_broadcast([P, H, HD]), ALU.mult).then_inc(attn_ready, 1)

            def moments(source, c0):
                for t in range(NT):
                    v.bn_stats(stats[:, c0 + t, :], source[:, t, :])

            def ahead(i, h, par, s):
                if s == -1:
                    dve.wait_ge(ld_x[par], 16)
                    moments(x_sb[:, par, :, :], i * NT)
                if s == 4:
                    dve.wait_ge(ld_x[par], h * 16 + 16)
                    moments(x_sb[:, par, :, :], NT)

            def root(i, h, par, s):
                if s in (-1, 4):
                    dve.drain()
                    for t in range(2 * NT):
                        v.bn_aggr(mv[:, t, :], stats[:, t, :])
                    dve.drain()
                    v.tensor_scalar(var[:], mv[:, :, 1], EPS, None, ALU.add)
                    dve.drain()
                    v.tensor_scalar(guess[:].bitcast(I32), var[:].bitcast(I32), 1, None, ALU.logical_shift_right)
                    dve.drain()
                    if s == 4:
                        wait(dve, xn_ready, min(i + 2, B) if isinstance(i, int) else i + 2)
                        wait(dve, xn2_ready, i - 1)
                    v.tensor_scalar(rstd[:].bitcast(I32), guess[:].bitcast(I32), -1.0, RSQRT_SEED, ALU.mult, ALU.add)
                for _ in range({-1: 3, 5: 1, 6: 2}.get(s, 0)):
                    dve.drain()
                    v.tensor_tensor(guess[:], rstd[:], rstd[:], ALU.mult)
                    dve.drain()
                    v.scalar_tensor_tensor(guess[:], guess[:], -0.5, var[:], ALU.mult, ALU.mult)
                    dve.drain()
                    v.scalar_tensor_tensor(rstd[:], guess[:], 1.5, rstd[:], ALU.add, ALU.mult)
                if s in (-1, 6):
                    dve.drain()
                    v.scalar_tensor_tensor(shift[:], mv[:, :, 0], -1.0, rstd[:], ALU.mult,
                                           ALU.mult).then_inc(root_ready, 1)

            def stage1(i, h, par, s):
                if s in (2, 7):
                    t = (s == 7) + 0
                    if t == 0:
                        wait(dve, qk_ready, i * NT)
                        wait(dve, pv_done, (i - 1) * U)
                    dve.wait_ge(ld_rotary, 2 * 16)
                    dve.wait_ge(qkv_ready, i * NT + (t + 1))
                    ps = (psB, psA)[t][:, 0:QK]
                    v.tensor_tensor(rot_a[:, t, :], ps, cos_sb[:, t, :], ALU.mult)
                    halves = ps.rearrange("p (h two e) -> p h two e", two=2, e=HD // 2)
                    turned = rot_b[:, t, :].rearrange("p (h two e) -> p h two e", two=2, e=HD // 2)
                    sines = sin_sb[:, t, :].rearrange("p (h two e) -> p h two e", two=2, e=HD // 2)
                    for w in range(2):
                        last = v.tensor_tensor(turned[:, :, w, :], halves[:, :, 1 - w, :],
                                               sines[:, :, w, :], ALU.mult)
                    last.then_inc(rot_ready, 1)
                    v.tensor_copy(v1[:, par, t, 0:HD], (psB, psA)[t][:, QK:QKV]).then_inc(v_ready, 1)

            def stage3(i, h, par, s):
                if s == 3:
                    dve.wait_ge(proj_ready, i + 1)
                    dve.wait_ge(xb_ready, i + 1)
                    dve.wait_ge(x2_stored[par], h * 16 + 16)
                    v.tensor_tensor(x2[:, par, :, :], psC[:].rearrange("p (t n) -> p t n", t=NT),
                                    xb[:, par, :, :], ALU.add).then_inc(x2_ready, 1)
                    wait(dve, row_free, i)
                    v.tensor_copy(row_sb[:, par, :, ID].bitcast(I32), token[:])
                    dve.drain()
                    v.tensor_scalar(token[:], token[:], float(S), None, ALU.add)
                if s == 4:
                    moments(x2[:, par, :, :], 0)
                if s == 8:
                    dve.wait_ge(logits_ready, i + 1)
                    v.reduce_max(neg_top[:], psC[:, 0:NT * E].rearrange("p (t e) -> p t e", t=NT), AX.X,
                                 negate=True).then_inc(top_ready, 1)
                if s == 9:
                    dve.wait_ge(exp_ready, i + 1)
                    v.reciprocal(esum[:], esum[:])
                    dve.drain()
                    pr = row_sb[:, par, :, PR:PR + E]
                    v.tensor_tensor(pr, eprob[:], esum[:].unsqueeze(2).to_broadcast([P, NT, E]), ALU.mult)
                    dve.drain()
                    for t in range(NT):
                        v.max(top8[:, t, :], pr[:, t, :])
                    dve.drain()
                    for t in range(NT):
                        v.match_replace(marked[:, t, :], top8[:, t, :], pr[:, t, :], -1.0)
                    dve.drain()
                    v.tensor_scalar(chosen[:], marked[:], 0.0, None, ALU.is_lt).then_inc(chosen_ready, 1)
                if s == 10:
                    dve.wait_ge(rank_ready, i + 1)
                    for t in range(NT):
                        ranks = psC[:, (1 + t) * 2 * E:(2 + t) * 2 * E]
                        v.tensor_tensor(slot[:, t, :], ranks[:, 0:E], next_row[:], ALU.add)
                        dve.drain()
                        v.tensor_tensor(next_row[:], next_row[:], ranks[:, E:2 * E], ALU.add)
                        v.tensor_tensor(slot[:, t, :], slot[:, t, :], chosen[:, t, :], ALU.mult)
                        dve.drain()
                        v.max(slot8[:, t, :], slot[:, t, :])
                    dve.drain()
                    v.tensor_copy(slot_ix[:, par, :, :], slot8[:]).then_inc(slots_ready, 1)

            run_phase1(dve, score, turn, weigh, stage3, stage1, ahead, root)

            v.tensor_tensor(n_row[:], next_row[0:1, :], region_row[0:1, :], ALU.subtract).then_inc(tb_dve, 1)
            dve.wait_ge(tb_pe, 1)
            v.tensor_scalar(over[:], psA[0:E, 0:1], -float(SLOTS), 0.0, ALU.add, ALU.max)
            dve.drain()
            v.tensor_scalar(over_i[:], over[:], float(P - 1), None, ALU.add)
            dve.drain()
            v.tensor_scalar(over_i[:], over_i[:], P.bit_length() - 1, None, ALU.logical_shift_right)
            dve.drain()
            v.tensor_scalar(over_base[:], psA[0:E, 0:1], region_col[0:E, :], -float(SLOTS + P), ALU.add, ALU.add)
            v.tensor_copy(over[:], over_i[:]).then_inc(tb_dve, 1)
            dve.wait_ge(tb_pe, 2)
            v.tensor_copy(over_start[:], psA[0:E, 2:3])
            dve.drain()
            v.tensor_tensor(over_end[:], over_start[:], over[:], ALU.add)
            v.scalar_tensor_tensor(over_base[:], over_start[:], float(P), over_base[:], ALU.mult, ALU.add)
            dve.drain()
            v.tensor_scalar(ended[:], tile_no[:], over_end[:, 0:1], None, ALU.is_ge)
            v.tensor_scalar(begun[:], tile_no[:], over_start[:, 0:1], None, ALU.is_ge)
            dve.drain()
            v.tensor_tensor(begun[:], begun[:], ended[:], ALU.subtract).then_inc(tb_dve, 1)
            v.tensor_scalar(table[:, MAIN:MAIN + E], next_row[0:1, :], -float(SLOTS), None, ALU.add)
            v.tensor_scalar(row_tmp[:], tile_no[0:1, :], -float(P), None, ALU.mult)
            dve.wait_ge(tb_pe, 3)
            dve.drain()
            v.tensor_copy(table[:, N_OVER:N_OVER + 1], psA[0:1, 4:5])
            v.tensor_scalar(table[:, OV_E:OV_E + OVW], psB[0:1, 0:OVW], float(E - 1), None, ALU.min)
            v.tensor_tensor(row_tmp[:], row_tmp[:], psC[0:1, 0:OVW], ALU.add)
            dve.drain()
            v.tensor_scalar(table[:, OV_ROW:OV_ROW + OVW], row_tmp[:], 0.0, None, ALU.max)
            dve.drain()
            v.tensor_copy(n_row[:], next_row[0:1, :]).then_inc(table_ready, 1)
            dve.wait_ge(table_ready, 1)

            def load(n, q, j, nsub, e, extra_no, n_over):
                if e is None:
                    e = dve.value_load(table[0:1, bass.ds(extra_no + OV_E, 1)], min_val=0, max_val=E - 1)
                dve.wait_ge(x_loaded[j], q * 16 + 16)
                v.tensor_copy(pcol[:, j, 0:nsub], xt[:, j, 0:nsub, bass.ds(e + PR, 1)].rearrange("p a o -> p (a o)")
                              ).then_inc(pcol_ready, 1)

            def up(n, q, j, nsub):
                dve.wait_ge(gate_ready, n + 1)
                wait(dve, down_ready, n - 1)
                v.tensor_tensor(hid[:, j % 2, 0:nsub * P], gate[:, j % 2, 0:nsub * P],
                                psG[j % 2][:, SLOTS:SLOTS + nsub * P], ALU.mult).then_inc(hid_ready, 1)

            def down(n, q, j, nsub):
                dve.wait_ge(down_ready, n + 1)
                dve.wait_ge(pcol_ready, n + 1)
                v.tensor_scalar(y[:, j, 0, :], psY[0][j % 2][:, 0:D], pcol[:, j, 0:1], None, ALU.mult).then_inc(y_dve, 1)

            run_phase2(dve, load, up, down)

        @block.tensor
        def _(pe):
            mm, tp = nc.tensor.matmul, nc.tensor.transpose
            pe.wait_ge(ld_consts, 16)
            pe.wait_ge(made_consts, 1)
            pe.wait_ge(made_ones, 4)

            def keep_warm(n):
                for _ in range(n):
                    mm(psS[0][:], ones_bf[:], mask_bf[:].rearrange("p h k -> p (h k)"), start=True, stop=True)

            keep_warm(WARM_START)

            def transpose_tiles(ps, source):
                for t in range(NT):
                    for c in range(2):
                        last = tp(ps[:, c * S + t * P:c * S + (t + 1) * P], source[:, t, c * P:(c + 1) * P], ident)
                return last

            def score(i, h, par, u):
                n, (t, h0, nh, nk) = i * U + u, unit_shape(u)
                if u == 0:
                    pe.wait_ge(qT_ready, i + 1)
                if u <= 1:
                    pe.wait_ge(kbd_ready, i * 2 + (u + 1))
                wait(pe, probs_ready, n - 1)
                g0 = h0 % G
                mm(psS[u % 2][:].rearrange("p (h k) -> p h k", h=nh), qT[:, par, h0 // G, t * P:(t + 1) * P],
                   kbd[:, par, g0:g0 + nh, 0:nk], start=True, stop=False)
                mm(psS[u % 2][:].rearrange("p (h k) -> p h k", h=nh)[:, :, nk - P:nk], ident_bf[:],
                   mask_bf[:, 0:nh, :], start=False, stop=True).then_inc(scores_ready, 1)

            def turn(i, h, par, u):
                n = i * U + u
                if isinstance(n, int) and n == B * U - 1:
                    keep_warm(2 * WARM_STEP)
                pe.wait_ge(probs_ready, n + 1)
                wait(pe, (pT_dve, pT_act)[u % 2], i * (U // 2) + u // 2)
                for k in range(4):
                    last = tp(psT[u % 2][:, k * P:(k + 1) * P], probs[:, u % 2, k * P:(k + 1) * P], ident)
                last.then_inc(pT_in, 1)

            def weigh(i, h, par, u):
                t, h0, nh, nk = unit_shape(u)
                pe.wait_ge((pT_dve, pT_act)[u % 2], i * (U // 2) + (u // 2 + 1))
                if u == 0:
                    pe.wait_ge(v_ready, i * NT + NT)
                if u in (0, 4):
                    wait(pe, attn_ready, i * NT + t)
                for k in range(nh):
                    for kt in range(t + 1):
                        block_no = k * (t + 1) + kt
                        last = mm(psO[:, (h0 + k) * VW:(h0 + k + 1) * VW],
                                  pT[:, u % 2, block_no * P:(block_no + 1) * P], v1[:, par, kt, :],
                                  start=(kt == 0), stop=(kt == t))
                last.then_inc(pv_done, 1)

            def stage1(i, h, par, s):
                if s == 0:
                    pe.wait_ge(xn_ready, i + 1)
                    wait(pe, qT_ready, i)
                    transpose_tiles(psA, xn[:, par, :, :]).then_inc(xnT_in, 1)
                if s == 1:
                    pe.wait_ge(ld_qkv, 16)
                    pe.wait_ge(xnT_ready, i + 1)
                    wait(pe, kbd_ready, i * 2)
                    for t in range(NT):
                        for c in range(2):
                            last = mm((psB, psA)[t][:, 0:QKV], xnT[:, c, t * P:(t + 1) * P], wqkv_sb[:, c, :],
                                      start=(c == 0), stop=(c == 1))
                        last.then_inc(qkv_ready, 1)
                if s == 9:
                    if isinstance(i, int) and i == 0:
                        keep_warm(WARM_ROTARY)
                    pe.wait_ge(qk_ready, i * NT + NT)
                    pe.wait_ge(v_ready, i * NT + NT)
                    for t in range(NT):
                        last = tp(psB[:, t * P:(t + 1) * P], krep[:, t, :, :].rearrange("p g w -> p (g w)"), ident)
                    transpose_tiles(psA, qk).then_inc(qkT_in, 1)

            def stage3(i, h, par, s):
                last_batch = isinstance(i, int) and i == B - 1
                if s == 2:
                    pe.wait_ge(attn_ready, i * NT + NT)
                    wait(pe, slots_ready, i)
                    transpose_tiles(psC, attn).then_inc(attnT_in, 1)
                if s == 3:
                    if last_batch:
                        keep_warm(WARM_STEP)
                    pe.wait_ge(ld_rest, 3 * 16)
                    pe.wait_ge(attnT_ready, i + 1)
                    for t in range(NT):
                        for c in range(2):
                            last = mm(psC[:, t * D:(t + 1) * D], attnT[:, c, t * P:(t + 1) * P], wproj_sb[:, c, :],
                                      start=(c == 0), stop=(c == 1))
                    last.then_inc(proj_ready, 1)
                if s == 7:
                    if last_batch:
                        keep_warm(WARM_ROOT)
                    pe.wait_ge(xn2_ready, i + 1)
                    transpose_tiles(psC, row_sb[:, par, :, :]).then_inc(xn2T_in, 1)
                if s == 8:
                    pe.wait_ge(xn2T_ready, i + 1)
                    for t in range(NT):
                        for c in range(2):
                            last = mm(psC[:, t * E:(t + 1) * E], xn2T[:, c, t * P:(t + 1) * P], wrouter_sb[:, c, :],
                                      start=(c == 0), stop=(c == 1))
                    last.then_inc(logits_ready, 1)
                if s == 10:
                    pe.wait_ge(chosen_ready, i + 1)
                    for t in range(NT):
                        c0 = (1 + t) * 2 * E
                        mm(psC[:, c0:c0 + E], tri[:], chosen[:, t, :], start=True, stop=True)
                        last = mm(psC[:, c0 + E:c0 + 2 * E], ones_bf[:], chosen[:, t, :], start=True, stop=True)
                    last.then_inc(rank_ready, 1)

            run_phase1(pe, score, turn, weigh, stage3, stage1)

            pe.wait_ge(tb_dve, 1)
            mm(psA[0:E, 0:1], n_row[:], ones[0:1, :], start=True, stop=True).then_inc(tb_pe, 1)
            pe.wait_ge(tb_dve, 2)
            mm(psA[0:E, 2:3], tri_f[0:E, 0:E], over[:], start=True, stop=True).then_inc(tb_pe, 1)
            pe.wait_ge(tb_dve, 3)
            mm(psA[0:1, 4:5], ones[0:E, :], over[:], start=True, stop=True)
            mm(psB[0:1, 0:OVW], ones[0:E, :], ended[:], start=True, stop=True)
            mm(psC[0:1, 0:OVW], over_base[:], begun[:], start=True, stop=True).then_inc(tb_pe, 1)
            pe.wait_ge(table_ready, 1)
            pe.wait_ge(sent[1][0], B // 2 * TOPK * 16)
            keep_warm(WARM_UNITS)

            def load(n, q, j, nsub, e, extra_no, n_over):
                pe.wait_ge(x_loaded[j], q * 16 + 16)
                wait(pe, xtT_ready, n - 1)
                for a in range(nsub):
                    for c in range(2):
                        last = tp(psX[j % 2][:, c * S + a * P:c * S + (a + 1) * P], xt[:, j, a, c * P:(c + 1) * P], ident)
                last.then_inc(xtT_in, 1)

            def up(n, q, j, nsub):
                pe.wait_ge(w_loaded[j], q * 16 + 16)
                pe.wait_ge(xtT_ready, n + 1)
                wait(pe, hid_ready, n - 1)
                for gu in range(2):
                    for c in range(2):
                        last = mm(psG[j % 2][:, gu * SLOTS:gu * SLOTS + nsub * P],
                                  w_sb[:, j, c * 2 * F + gu * F:c * 2 * F + (gu + 1) * F],
                                  xtT[:, j % 2, c, 0:nsub * P], start=(c == 0), stop=(c == 1))
                last.then_inc(gu_ready, 1)

            def down(n, q, j, nsub):
                pe.wait_ge(hid_ready, n + 1)
                wait(pe, y_dve, n - 1)
                wait(pe, y_act, n - 1 if nsub == NT else E)
                for a in range(nsub):
                    last = mm(psY[a][j % 2][:, 0:D], hid[:, j % 2, a * P:(a + 1) * P],
                              w_sb[:, j, 4 * F:4 * F + D], start=True, stop=True)
                last.then_inc(down_ready, 1)

            run_phase2(pe, load, up, down)


def tables():
    import numpy as np

    f32 = np.float32
    inv_freq = (f32(1.0) / f32(10000.0) ** (np.arange(0, HD, 2, dtype=f32) / f32(HD))).astype(f32)
    t = np.arange(S, dtype=f32)
    freqs = np.einsum("i,j->ij", t, inv_freq).astype(f32)
    freqs = np.concatenate((freqs, freqs), axis=-1)
    base = ((np.arange(0, HD, 2, dtype=f32) + f32(0.4 * HD)) / f32(1.4 * HD)).astype(f32)
    power = ((t - S // 2) / 64).astype(f32)
    scale = (base[None, :] ** power[:, None]).astype(f32)
    scale = np.concatenate((scale, scale), axis=-1)
    sign = np.concatenate((-np.ones(HD // 2), np.ones(HD // 2))).astype(f32)
    weight = f32(HD ** -0.5)
    inverse = (f32(1.0) / scale).astype(f32)
    cos = np.concatenate([np.tile(np.cos(freqs) * scale, (1, H)), np.cos(freqs) * inverse], axis=1) * weight
    sin = np.concatenate([np.tile(np.sin(freqs) * scale * sign, (1, H)), np.sin(freqs) * inverse * sign], axis=1) * weight
    p = np.arange(P)
    consts = np.concatenate([
        np.eye(P), p[:, None] < p[None, :], np.where(p[None, :] > p[:, None], MASKED, 0.0),
        p[:, None] // HD == np.arange(G)[None, :],
        np.broadcast_to(np.arange(E) * REGION + PAD, (P, E)),
        (np.minimum(p, E - 1) * REGION + PAD)[:, None],
        p[:, None] + P * np.arange(NT)[None, :],
    ], axis=1)
    return cos.astype(f32), sin.astype(f32), consts.astype(f32)


def kernel(L0_attn_hidden_states, L0_attn_w_q, L0_attn_w_kv, L0_attn_w_proj, L0_attn_b_proj,
           L0_ffn_router_weight, L0_ffn_gate_up_proj, L0_ffn_down_proj):
    import numpy as np
    import concourse.bacc as bacc
    from concourse.bass_utils import run_bass_kernel_spmd as run

    a = np.asarray
    c = np.ascontiguousarray
    gu = a(L0_ffn_gate_up_proj).transpose(0, 2, 1).reshape(E, 2, P, 2 * F).transpose(0, 2, 1, 3).reshape(E, P, 4 * F)
    dn = a(L0_ffn_down_proj).transpose(0, 2, 1)
    cos, sin, consts = tables()
    arrays = {
        "x": c(a(L0_attn_hidden_states).reshape(T, D)),
        "wqkv": c(np.concatenate([a(L0_attn_w_q).T, a(L0_attn_w_kv).T], axis=1)),
        "wproj": c(a(L0_attn_w_proj).T),
        "bproj": c(a(L0_attn_b_proj)),
        "wrouter": c(a(L0_ffn_router_weight).T),
        "wexpert": c(np.concatenate([gu, dn], axis=2).reshape(E * P, WCOLS)),
        "cos": cos, "sin": sin, "consts": consts,
    }
    nc = bacc.Bacc("TRN2", target_bir_lowering=False, num_devices=1)
    args = [nc.dram_tensor(n, v.shape, F32, kind="ExternalInput").ap() for n, v in arrays.items()]
    out = nc.dram_tensor("out_0_dram", (T + PAD, D), F32, kind="ExternalOutput").ap()
    rows = nc.dram_tensor("rows", (E * REGION, ROW), F32, kind="Internal").ap()
    acc = [nc.dram_tensor(f"acc{i}", (T + PAD, D), F32, kind="Internal").ap() for i in (1, 2)]
    moe_block(nc, *args, out, rows, *acc)
    r = run(nc, [arrays], core_ids=[0])
    return r.results[0]["out_0_dram"][:T].reshape(B, S, D)
```
